# Optimizing a Trainium2 kernel written in Bass

```python
import numpy as np
import jax
import jax.numpy as jnp

def _softmax(x, axis=-1):
    return jax.nn.softmax(x, axis=axis)

def _gelu(x):
    return jax.nn.gelu(x, approximate=True)

def _silu(x):
    return jax.nn.silu(x)

def _sigmoid(x):
    return jax.nn.sigmoid(x)

def _layernorm(x, axis=-1, eps=1e-05):
    m = jnp.mean(x, axis=axis, keepdims=True)
    v = jnp.var(x, axis=axis, keepdims=True)
    return (x - m) / jnp.sqrt(v + eps)

def _scatter_add(tgt, idx, src, axis=0):
    return tgt.at[idx].add(src)

def _segment_sum(src, seg, n):
    return jax.ops.segment_sum(src, seg, n)
kernel_name = 'mk_recurrent_d1_jaxref_r8_d2db1f'

def setup_inputs(seed: int=0):
    np.random.seed(seed)
    _w = jnp.asarray

    def _L0_attn_setup():
        import jax, jax.numpy as jnp
        import numpy as np
        import math
        HIDDEN = 512
        NUM_HEADS = 32
        HEAD_DIM = HIDDEN // NUM_HEADS
        SCALE = 1.0 / HEAD_DIM

        def _alibi_slopes(n_heads: int) -> np.ndarray:
            cp2 = 2 ** math.floor(math.log2(n_heads))
            base = 2 ** (-2 ** (-(math.log2(cp2) - 3)))
            slopes = base ** np.arange(1, cp2 + 1, dtype=np.float32)
            if cp2 != n_heads:
                extra_base = 2 ** (-2 ** (-(math.log2(2 * cp2) - 3)))
                n_rem = min(cp2, n_heads - cp2)
                extra = extra_base ** np.arange(1, 1 + 2 * n_rem, 2, dtype=np.float32)
                slopes = np.concatenate([slopes, extra])
            return slopes.astype(np.float32)
        key = jax.random.key(seed)
        k1, k2, k3, k4, k5 = jax.random.split(key, 5)
        B, S = (2, 256)
        return {'hidden_states': jax.random.normal(k1, (B, S, HIDDEN), dtype=jnp.float32), 'w_attn': jax.random.normal(k2, (HIDDEN, 3 * HIDDEN), dtype=jnp.float32) * 0.02, 'b_attn': jnp.zeros((3 * HIDDEN,), dtype=jnp.float32), 'w_proj': jax.random.normal(k3, (HIDDEN, HIDDEN), dtype=jnp.float32) * 0.02, 'b_proj': jnp.zeros((HIDDEN,), dtype=jnp.float32)}
    _L0_attn_in = _L0_attn_setup()

    def _L0_ffn_setup():
        import jax, jax.numpy as jnp
        import numpy as np
        B, T, D_IN, D_OUT = (8, 256, 512, 512)
        N_LORAS, RANK = (16, 32)
        SCALING = 1.0
        key = jax.random.key(seed)
        ks = jax.random.split(key, 8)
        std = 1.0 / D_IN ** 0.5
        x = jax.random.normal(ks[0], (B, T, D_IN), dtype=jnp.float32)
        idx = jax.random.randint(ks[1], (B,), 0, N_LORAS)
        gate = jax.nn.one_hot(idx, N_LORAS, dtype=jnp.float32)
        kernel = jax.random.normal(ks[2], (D_IN, D_OUT), dtype=jnp.float32) * std
        bias = jnp.zeros((D_OUT,), dtype=jnp.float32)
        lora_A = jax.random.normal(ks[3], (N_LORAS, RANK, D_IN), dtype=jnp.float32) * std
        lora_B = jax.random.normal(ks[4], (N_LORAS, D_OUT, RANK), dtype=jnp.float32) * 0.01
        lora_A_shared = jax.random.normal(ks[5], (RANK, D_IN), dtype=jnp.float32) * std
        lora_B_shared = jax.random.normal(ks[6], (D_OUT, RANK), dtype=jnp.float32) * 0.01
        return {'x': x, 'gate': gate, 'kernel': kernel, 'bias': bias, 'lora_A': lora_A, 'lora_B': lora_B, 'lora_A_shared': lora_A_shared, 'lora_B_shared': lora_B_shared}
    _L0_ffn_in = _L0_ffn_setup()
    _d = {'L0_attn_hidden_states': _L0_attn_in['hidden_states'], 'L0_attn_w_attn': _L0_attn_in['w_attn'], 'L0_attn_b_attn': _L0_attn_in['b_attn'], 'L0_attn_w_proj': _L0_attn_in['w_proj'], 'L0_attn_b_proj': _L0_attn_in['b_proj'], 'L0_ffn_gate': _L0_ffn_in['gate'], 'L0_ffn_kernel': _L0_ffn_in['kernel'], 'L0_ffn_bias': _L0_ffn_in['bias'], 'L0_ffn_lora_A': _L0_ffn_in['lora_A'], 'L0_ffn_lora_B': _L0_ffn_in['lora_B'], 'L0_ffn_lora_A_shared': _L0_ffn_in['lora_A_shared'], 'L0_ffn_lora_B_shared': _L0_ffn_in['lora_B_shared']}
    _x0 = _d['L0_attn_hidden_states']
    _d['L0_attn_hidden_states'] = jax.random.normal(jax.random.fold_in(jax.random.key(seed), 1), (2, 1024, 512), dtype=_x0.dtype)
    del _x0
    return _d

def reference(L0_attn_hidden_states, L0_attn_w_attn, L0_attn_b_attn, L0_attn_w_proj, L0_attn_b_proj, L0_ffn_gate, L0_ffn_kernel, L0_ffn_bias, L0_ffn_lora_A, L0_ffn_lora_B, L0_ffn_lora_A_shared, L0_ffn_lora_B_shared):

    def _L0_attn_ref(hidden_states, w_attn, b_attn, w_proj, b_proj):
        import jax, jax.numpy as jnp
        import numpy as np
        import math
        HIDDEN = 512
        NUM_HEADS = 32
        HEAD_DIM = HIDDEN // NUM_HEADS
        SCALE = 1.0 / HEAD_DIM

        def _alibi_slopes(n_heads: int) -> np.ndarray:
            cp2 = 2 ** math.floor(math.log2(n_heads))
            base = 2 ** (-2 ** (-(math.log2(cp2) - 3)))
            slopes = base ** np.arange(1, cp2 + 1, dtype=np.float32)
            if cp2 != n_heads:
                extra_base = 2 ** (-2 ** (-(math.log2(2 * cp2) - 3)))
                n_rem = min(cp2, n_heads - cp2)
                extra = extra_base ** np.arange(1, 1 + 2 * n_rem, 2, dtype=np.float32)
                slopes = np.concatenate([slopes, extra])
            return slopes.astype(np.float32)
        B, S, _ = hidden_states.shape
        H, D = (NUM_HEADS, HEAD_DIM)
        qkv = hidden_states @ w_attn + b_attn
        q, k, v = jnp.split(qkv, 3, axis=-1)
        q = q.reshape(B, S, H, D)
        k = k.reshape(B, S, H, D)
        v = v.reshape(B, S, H, D)
        scores = jnp.einsum('bqhd,bkhd->bhqk', q, k) * SCALE
        slopes = jnp.asarray(_alibi_slopes(H))
        pos = jnp.arange(S)
        rel = pos[None, :] - pos[:, None]
        bias = slopes[:, None, None] * rel[None, :, :]
        causal = rel <= 0
        scores = jnp.where(causal[None, None], scores + bias[None], -jnp.inf)
        attn = jax.nn.softmax(scores, axis=-1)
        out = jnp.einsum('bhqk,bkhd->bqhd', attn, v).reshape(B, S, HIDDEN)
        return out @ w_proj + b_proj

    def _L0_ffn_ref(x, gate, kernel, bias, lora_A, lora_B, lora_A_shared, lora_B_shared):
        import jax, jax.numpy as jnp
        import numpy as np
        B, T, D_IN, D_OUT = (8, 256, 512, 512)
        N_LORAS, RANK = (16, 32)
        SCALING = 1.0
        base_out = jnp.matmul(x, kernel) + bias
        b = gate.shape[0]
        x_flat = x.reshape(b, -1, x.shape[-1])
        A_eff = jnp.einsum('bn,nri->bri', gate, lora_A)
        B_eff = jnp.einsum('bn,nor->bor', gate, lora_B)
        Ax = jnp.einsum('bri,bti->btr', A_eff, x_flat)
        delta_flat = jnp.einsum('bor,btr->bto', B_eff, Ax)
        Ax_s = jnp.einsum('ri,bti->btr', lora_A_shared, x_flat)
        delta_flat = delta_flat + jnp.einsum('or,btr->bto', lora_B_shared, Ax_s)
        delta = delta_flat.reshape(x.shape[:-1] + (kernel.shape[-1],))
        return base_out + (SCALING * delta).astype(base_out.dtype)
    x = L0_attn_hidden_states
    xn = _layernorm(x, axis=-1)
    s = _L0_attn_ref(xn, L0_attn_w_attn, L0_attn_b_attn, L0_attn_w_proj, L0_attn_b_proj)
    g = _silu(_L0_ffn_ref(xn, L0_ffn_gate, L0_ffn_kernel, L0_ffn_bias, L0_ffn_lora_A, L0_ffn_lora_B, L0_ffn_lora_A_shared, L0_ffn_lora_B_shared))
    x = x + s * g
    return x

_drawn_inputs = setup_inputs


def setup_inputs(seed=0):
    import zlib

    import numpy as np

    out = dict(_drawn_inputs(seed))
    spreads = {'L0_attn_b_attn': (0.0, 0.304), 'L0_attn_b_proj': (0.0, 0.1), 'L0_ffn_bias': (0.0, 2.0)}
    factors = {'L0_ffn_gate': 8.0,
     'L0_ffn_lora_A': 8.0,
     'L0_ffn_lora_B': 8.0,
     'L0_ffn_lora_A_shared': 29.329,
     'L0_ffn_lora_B_shared': 29.511,
     'L0_ffn_kernel': 8.0}
    for name, (base, spread) in spreads.items():
        noise = np.random.default_rng([zlib.crc32(name.encode()), seed]).standard_normal(out[name].shape)
        drawn = base * np.exp(spread * noise) if base else spread * noise
        out[name] = jnp.asarray(drawn.astype(out[name].dtype))
    for name, factor in factors.items():
        out[name] = (out[name] * factor).astype(out[name].dtype)
    return out
```

```python
from contextlib import ExitStack

import concourse.bass as bass
from concourse import mybir

F32 = mybir.dt.float32
BF16 = mybir.dt.bfloat16
ALU = mybir.AluOpType
AX = mybir.AxisListType
ACT = mybir.ActivationFunctionType

P = 128
BATCH, SEQ, HID = 2, 1024, 512
TOK = BATCH * SEQ
HEADS = 32
HD = HID // HEADS
KT = HID // P
HG = 4
DT_HEADS = P // HD
DTS = HEADS // DT_HEADS
STEPS = 4
CH = 512
CHUNKS = SEQ // CH
QT = SEQ // P
CT = CH // P
PIECES = 3
PROD = 6 * HD
ALIBI0 = PROD
NEGMAX0 = PROD + PIECES
ROWS_MAX = NEGMAX0
ROWS_ALL = NEGMAX0 + PIECES
Q_PIECES = [0, 0, 0, 1, 1, 2]
K_PIECES = [0, 1, 2, 0, 1, 0]
SCALE = 1.0 / HD
NEG = -3.0e38
EPS = 1e-5
VC = 2 * HD

LORAS, RANK, GROUPS = 16, 32, 8
GTOK = TOK // GROUPS
NR = LORAS * RANK
RC = 2 * RANK

UNITS = [(c, kb) for c in range(CHUNKS) for kb in range(CT * (c + 1))]
NU = len(UNITS)
MAXES = [(h, t, c) for h in range(HG) for t in range(QT) for c in range(t // CT + 1)]
NM = len(MAXES)
PER_UNIT = 5


def width(n):
    c, kb = UNITS[n]
    return CH - max(0, kb - CT * c) * P


def diagonal(n):
    c, kb = UNITS[n]
    return kb >= CT * c


def maxes_of(n):
    return range(PER_UNIT * n, min(PER_UNIT * (n + 1), NM))


def keys_of(t, c):
    return min(CH, (t + 1) * P - c * CH)


class Tally:

    def __init__(self, n=0):
        self.n = n

    def add(self, k=1):
        self.n += k
        return self.n

    def back(self, trip, less=0, rate=0):
        v = self.n - less
        return v if isinstance(trip, int) else trip * rate + v


def attention_and_gate(nc, x, w_qk, w_v, b_qk, b_v, w_proj, b_proj, gate, w_ffn, b_ffn, lora_a, lora_b,
                       lora_as, lora_bs, ident_d, identb_d, mask_d, maskb_d, alibi_d, pick_d, out):
    ctx = ExitStack()
    with ctx:
        def sb(name, shape, dt):
            return ctx.enter_context(nc.sbuf_tensor(name, shape, dt))

        def sem(name):
            return ctx.enter_context(nc.semaphore(name))

        sums_d = nc.dram_tensor("sums_d", [HEADS, TOK], F32, kind="Internal").ap()
        inv_d = nc.dram_tensor("inv_d", [HEADS, TOK], F32, kind="Internal").ap()
        acat_d = nc.dram_tensor("acat_d", [P, KT * GROUPS * RC], F32, kind="Internal").ap()
        bcat_d = nc.dram_tensor("bcat_d", [RC, GROUPS, HID], F32, kind="Internal").ap()

        xnT = sb("xnT", [P, KT, TOK], F32)
        att = sb("att", [P, KT, TOK], F32)
        qs = [sb(f"qs{i}", [P, HG, SEQ], BF16) for i in range(STEPS)]
        ks = [sb(f"ks{i}", [P, HG, SEQ], BF16) for i in range(STEPS)]
        va = [sb(f"va{b}", [P, QT, DT_HEADS, VC], F32) for b in range(BATCH)]
        probs = [sb(f"probs{i}", [P, HG, CH], F32) for i in range(3)]
        wqk = [sb(f"wqk{g}", [P, KT, P], F32) for g in range(2)]
        wv = sb("wv", [P, KT, P], F32)
        bqk = [sb(f"bqk{g}", [P, 1], F32) for g in range(2)]
        qk = sb("qk", [P, SEQ], F32)
        pieces = sb("pieces", [P, PIECES, SEQ], BF16)
        raw = [sb(f"raw{c}", [P, CH], F32) for c in range(CHUNKS)]
        mask = sb("mask", [P, CH], F32)
        ident = sb("ident", [P, P], F32)
        maskb = sb("maskb", [P, P], BF16)
        identb = sb("identb", [P, P], BF16)
        junk = sb("junk", [P, 2, CH], BF16)
        tops = sb("tops", [P, CHUNKS, HG * QT], F32)
        top = sb("top", [P, HG * QT], F32)
        toprest = sb("toprest", [P, HG * QT], F32)
        negmax = sb("negmax", [P, PIECES, HG * QT], BF16)
        negmaxT = sb("negmaxT", [PIECES * HG * QT, P], BF16)
        bv = sb("bv", [P, KT], F32)
        stats = sb("stats", [P, 4, 6], F32)
        meanvar = sb("meanvar", [P, 4, 2], F32)
        std = sb("std", [P, 4], F32)
        rstd = sb("rstd", [P, 4], F32)

        def pb(name, shape):
            return ctx.enter_context(nc.psum_tensor(name, shape, F32))

        mxp = [pb(f"mxp{i}", [P, CH]) for i in range(2)]
        stp = [pb(f"stp{i}", [P, 2, CH]) for i in range(2)]
        accp = pb("accp", [P, CH])
        miscp = pb("miscp", [P, CH])

        s_ident = sem("s_ident")
        s_const = sem("s_const")
        s_x = [sem(f"s_x{i}") for i in range(4)]
        s_init = sem("s_init")
        s_stats = sem("s_stats")
        s_var = sem("s_var")
        s_std = sem("s_std")
        s_rstd = sem("s_rstd")
        s_xn = sem("s_xn")
        s_xt = sem("s_xt")
        s_xte = sem("s_xte")
        s_w = [sem(f"s_w{g}") for g in range(2)]
        s_wv = sem("s_wv")
        s_misc = sem("s_misc")
        s_hi = sem("s_hi")
        s_v = sem("s_v")
        s_mid = sem("s_mid")
        s_rest = sem("s_rest")
        s_lo = sem("s_lo")
        s_stack = sem("s_stack")
        s_mx = sem("s_mx")
        s_mx_free = sem("s_mx_free")
        s_top = sem("s_top")
        s_neg = sem("s_neg")
        s_negT = sem("s_negT")
        s_negrows = sem("s_negrows")
        s_scores = sem("s_scores")
        s_exp = sem("s_exp")
        s_seen = sem("s_seen")
        s_pv = sem("s_pv")
        s_acc_free = sem("s_acc_free")
        s_raw = [sem(f"s_raw{c}") for c in range(CHUNKS)]

        def f32view(t):
            return t[:, :, :].rearrange("p a b -> p (a b)").bitcast(F32)

        xin = [probs[0], probs[1]]
        la = f32view(qs[0]).rearrange("p (k i) -> p k i", k=KT)
        lbr = f32view(qs[1]).rearrange("p (c m) -> p c m", c=KT)
        lbT = f32view(qs[2]).rearrange("p (c m) -> p c m", c=KT)
        gsel = f32view(qs[3])[:, 0:KT * GROUPS * RANK]
        acat = f32view(ks[0]).rearrange("p (k g r) -> p k g r", k=KT, g=GROUPS)
        beff = f32view(ks[1])[:, 0:2 * HID].rearrange("p (a o) -> p a o", a=2)
        las = f32view(ks[1])[0:RANK, 2 * HID:3 * HID]
        lbsr = f32view(ks[2])[:, 0:KT * RANK].rearrange("p (c r) -> p c r", c=KT)
        pick = f32view(ks[2])[:, 256:256 + RANK]
        gatep = f32view(ks[2])[:, 512:512 + KT * GROUPS]
        gateall = f32view(ks[2])[:, 640:640 + GROUPS * LORAS]
        lbsT = f32view(ks[2])[0:RANK, 1024:1024 + HID]
        s_lora = sem("s_lora")
        s_gsel = sem("s_gsel")
        s_lp = sem("s_lp")
        s_le = sem("s_le")
        s_lst = sem("s_lst")

        wf = f32view(qs[0]).rearrange("p (k o) -> p k o", k=KT)
        acat2 = f32view(ks[0]).rearrange("p (k m) -> p k m", k=KT)
        bcat2 = [f32view(t)[0:RC, :].rearrange("p (g o) -> p g o", g=4) for t in (qs[1], ks[1])]
        invb = [f32view(t) for t in (qs[2], ks[2])]
        wp = f32view(qs[3]).rearrange("p (k o) -> p k o", k=KT)
        axT = f32view(ks[3])
        sums = qk[:, 0:CH]
        inv = qk[:, CH:2 * CH]
        xt = probs
        bfb = raw[0]
        bpb = raw[1]
        va_f = [t[:, :, :, :].rearrange("p a b c -> p (a b c)") for t in va]
        NG = 5
        g_t = [va_f[0][:, i * HID:(i + 1) * HID] for i in range(4)] + [wv[:, :, :].rearrange("p a b -> p (a b)")]
        z_t = [va_f[1][:, i * HID:(i + 1) * HID] for i in range(2)]
        y_t = [va_f[1][:, i * HID:(i + 1) * HID] for i in range(2, 4)]
        s_f0 = sem("s_f0")
        s_bc = sem("s_bc")
        s_wp = sem("s_wp")
        s_sums = sem("s_sums")
        s_inv = sem("s_inv")
        s_invst = sem("s_invst")
        s_invb = [sem(f"s_invb{i}") for i in range(2)]
        s_am = sem("s_am")
        s_att = sem("s_att")
        s_xl = [sem(f"s_xl{i}") for i in range(3)]
        s_fb = sem("s_fb")
        s_ax = sem("s_ax")
        s_axe = sem("s_axe")
        s_ff = sem("s_ff")
        s_z = sem("s_z")
        s_g = sem("s_g")
        s_op = sem("s_op")
        s_y = sem("s_y")
        s_yg = sem("s_yg")
        s_res = sem("s_res")
        s_out = [sem(f"s_out{i}") for i in range(2)]

        block = ctx.enter_context(nc.Block())

        def dt_of(trip, ahead):
            return trip + ahead // STEPS

        @block.sync
        def _(sp):
            sp.dma_start(ident[:, :], ident_d).then_inc(s_ident, 16)
            for i in range(4):
                if i >= 2:
                    sp.wait_ge(s_xn, i - 1)
                    sp.wait_ge(s_xt, 4 * (i - 1))
                sp.dma_start(xin[i % 2][:, :, :],
                             x[i * 4 * P:(i + 1) * 4 * P, :].rearrange("(t p) d -> p t d", p=P)).then_inc(s_x[i], 16)
                if i == 1:
                    sp.dma_start(la, lora_a.rearrange("n r i -> (n r) i").rearrange("(k p) i -> p k i", p=P)).then_inc(s_lora, 16)
                    sp.dma_start(lbr.rearrange("p c (n r) -> p c n r", r=RANK)[:, 0],
                                 lora_b[:, 0:P, :].rearrange("n o r -> o n r")).then_inc(s_lora, 16)
                    for c in range(1, KT):
                        sp.dma_start(lbr.rearrange("p c (n r) -> p c n r", r=RANK)[:, c],
                                     lora_b[:, c * P:(c + 1) * P, :].rearrange("n o r -> o n r")).then_inc(s_lora, 16)
                    sp.dma_start(las, lora_as).then_inc(s_lora, 16)
                    sp.dma_start(lbsr, lora_bs.rearrange("(c p) r -> p c r", p=P)).then_inc(s_lora, 16)
                    sp.dma_start(pick, pick_d).then_inc(s_lora, 16)
                    sp.dma_start(gateall, bass.AP(tensor=gate.tensor, offset=gate.offset,
                                                  ap=[[0, P], [1, GROUPS * LORAS]])).then_inc(s_lora, 16)
            sp.dma_start(identb[:, :], identb_d).then_inc(s_const, 16)
            sp.dma_start(mask[:, :], mask_d).then_inc(s_const, 16)
            sp.dma_start(maskb[:, :], maskb_d).then_inc(s_const, 16)
            sp.dma_start(bv[:, :], b_v).then_inc(s_const, 16)

            def load_wqk(g, dt):
                sp.dma_start(wqk[g][:, :, :], w_qk[bass.ds(dt * 2 + g, 1)].rearrange("g (k p) n -> p (g k) n", p=P))\
                  .then_inc(s_w[g], 16)
                sp.dma_start(bqk[g][:, :], b_qk[bass.ds(dt * 2 + g, 1)].rearrange("g p -> p g"),
                             allow_slow_non_contiguous=True).then_inc(s_w[g], 16)

            def load_wv(dt):
                sp.dma_start(wv[:, :, :], w_v.rearrange("(k p) n -> p k n", p=P)[:, :, bass.ds(dt * P, P)]).then_inc(s_wv, 16)

            load_wqk(0, 0)
            load_wv(0)
            load_wqk(1, 0)

            sp.wait_ge(s_le, 4 + 1)
            sp.dma_start(acat_d, f32view(ks[0])).then_inc(s_lst, 16)
            sp.wait_ge(s_le, 4 + 1 + 4 + 1 + 2)
            for g in range(GROUPS):
                sp.dma_start(bcat_d[0:RANK, g, :], beff[(g % 4) * RANK:(g % 4 + 1) * RANK, g // 4, :]).then_inc(s_lst, 16)
                sp.dma_start(bcat_d[RANK:RC, g, :], lbsT).then_inc(s_lst, 16)

            pieced = Tally()
            negs = Tally()
            stacked = Tally()
            accs = Tally()
            done = Tally()

            def stack(trip, ahead):
                u = ahead % STEPS
                pieced.add()
                sp.wait_ge(s_hi, pieced.back(trip, 0, STEPS) * CHUNKS)
                sp.wait_ge(s_lo, pieced.back(trip, 0, STEPS))
                for a, (tile, order) in enumerate(((qs[u], Q_PIECES), (ks[u], K_PIECES))):
                    for r, piece in enumerate(order):
                        sp.dma_start(tile[r * HD:(r + 1) * HD, :, :],
                                     pieces[a * 64:(a + 1) * 64, piece, :]).then_inc(s_stack, 16)
                group = 2 * dt_of(trip, ahead) + u % 2
                sp.dma_start(ks[u][ALIBI0:ALIBI0 + PIECES, :, :].rearrange("p h n -> p (h n)"),
                             alibi_d[bass.ds(group, 1)].rearrange("g p n -> (g p) n")).then_inc(s_stack, 16)

            def neg_rows(trip, ahead):
                u = ahead % STEPS
                negs.add()
                sp.wait_ge(s_negT, negs.back(trip, 0, STEPS))
                sp.dma_start(qs[u][NEGMAX0:ROWS_ALL, :, :], negmaxT[:, :]).then_inc(s_negrows, 16)

            def store_raw(trip, u, c):
                accs.add()
                dt = dt_of(trip, u)
                g, b = u % 2, u // 2
                sp.wait_ge(s_acc_free, accs.back(trip, 0, 2 * STEPS) + 1)
                at = b * SEQ + c * CH
                sp.dma_start(att[g * 64:(g + 1) * 64, bass.ds(dt, 1), at:at + CH],
                             raw[c][0:P:2, :]).then_inc(s_raw[c], 16)
                sp.dma_start(sums_d[bass.ds(dt * DT_HEADS + g * HG, HG), at:at + CH],
                             raw[c][1:P:VC, :]).then_inc(s_raw[c], 16)

            sp.wait_ge(s_lst, 16 * (1 + 2 * GROUPS))
            sp.wait_ge(s_init, 1)
            stack(0, 0)
            stack(0, 1)
            neg_rows(0, 0)
            for c in range(CHUNKS):
                sp.sem_inc(s_raw[c], 32)

            def step(trip, u, last):
                done.add()
                if not (last and u >= 2):
                    stack(trip, u + 2)
                if not last:
                    if u == 1:
                        sp.wait_ge(s_pv, done.back(trip, 1, STEPS) * NU + 3)
                        load_wqk(0, dt_of(trip, STEPS))
                        load_wv(dt_of(trip, STEPS))
                    if u == 2:
                        sp.wait_ge(s_pv, done.back(trip, 1, STEPS) * NU + 3)
                        load_wqk(1, dt_of(trip, STEPS))
                store_raw(trip, u, 0)
                if not (last and u == 3):
                    neg_rows(trip, u + 1)
                store_raw(trip, u, 1)

            with sp.Fori(0, DTS - 1, 1) as trip:
                for u in range(STEPS):
                    step(trip, u, False)
            for t in (pieced, negs, done):
                t.n += STEPS * (DTS - 2)
            accs.n += 2 * STEPS * (DTS - 2)
            for u in range(STEPS):
                step(DTS - 1, u, True)
                sp.wait_ge(s_pv, 3 + NU * done.n)
                if u == 0:
                    sp.dma_start(acat2.rearrange("p k m -> p (k m)"), acat_d).then_inc(s_f0, 16)
                    sp.dma_start(wf, w_ffn.rearrange("(k p) o -> p k o", p=P)).then_inc(s_f0, 16)
                if u == 1:
                    for j in range(2):
                        sp.dma_start(bcat2[j], bcat_d[:, 4 * j:4 * j + 4, :]).then_inc(s_bc, 16)
                if u == 3:
                    sp.dma_start(wp, w_proj.rearrange("(k p) o -> p k o", p=P)).then_inc(s_wp, 16)
            for c in range(CHUNKS):
                sp.wait_ge(s_raw[c], 32 * (1 + STEPS * DTS))
            sp.dma_start(sums, sums_d.rearrange("h (a n) -> (h a) n", n=CH)).then_inc(s_sums, 16)
            sp.dma_start(bfb[:, :], bass.AP(tensor=b_ffn.tensor, offset=b_ffn.offset, ap=[[0, P], [1, HID]])).then_inc(s_fb, 16)
            sp.dma_start(bpb[:, :], bass.AP(tensor=b_proj.tensor, offset=b_proj.offset, ap=[[0, P], [1, HID]])).then_inc(s_fb, 16)
            sp.wait_ge(s_pv, 3 + NU * STEPS * DTS)
            for i in range(3):
                sp.dma_start(xt[i][:, :, :], x[i * 4 * P:(i + 1) * 4 * P, :].rearrange("(t p) d -> p t d", p=P)).then_inc(s_xl[i], 16)
            sp.wait_ge(s_inv, 1)
            sp.dma_start(inv_d.rearrange("h (a n) -> (h a) n", n=CH), inv).then_inc(s_invst, 16)
            sp.wait_ge(s_invst, 16)
            for dt in range(DTS):
                if dt >= 2:
                    sp.wait_ge(s_am, dt - 1)
                src = inv_d[dt * DT_HEADS:(dt + 1) * DT_HEADS, :]
                sp.dma_start(invb[dt % 2], bass.AP(tensor=src.tensor, offset=src.offset,
                                                   ap=[[TOK, DT_HEADS], [0, HD], [1, TOK]])).then_inc(s_invb[dt % 2], 16)
            for i in range(TOK // P):
                if i == 4:
                    sp.dma_start(xt[0][:, :, :], x[12 * P:16 * P, :].rearrange("(t p) d -> p t d", p=P)).then_inc(s_xl[0], 16)
                sp.wait_ge(s_res, i + 1)
                sp.dma_start(out[i * P:(i + 1) * P, :], y_t[i % 2]).then_inc(s_out[i % 2], 16)
            for j in range(2):
                sp.wait_ge(s_out[j], 16 * (TOK // P // 2))

        def lora_prep(pe):
            uses = [0]
            banks = [mxp[0], mxp[1], accp, miscp]

            def bank():
                n = uses[0]
                if n >= 4:
                    pe.wait_ge(s_le, n - 3)
                uses[0] += 1
                return banks[n % 4]

            pe.wait_ge(s_lora, 16 * 9)
            pe.wait_ge(s_gsel, 2)
            for it in range(KT):
                b = bank()
                for k in range(KT):
                    m = pe.matmul(b[:, 0:GROUPS * RANK], la[:, k, it * P:(it + 1) * P], gsel[:, k * 256:(k + 1) * 256],
                                  start=(k == 0), stop=(k == KT - 1))
                m.then_inc(s_lp, 1)
            b = bank()
            for it in range(KT):
                m = pe.transpose(b[:, it * RANK:(it + 1) * RANK], las[:, it * P:(it + 1) * P], ident[0:RANK, 0:RANK])
            m.then_inc(s_lp, 1)
            for k in range(KT):
                b = bank()
                for c in range(KT):
                    m = pe.transpose(b[:, c * P:(c + 1) * P], lbr[:, c, k * P:(k + 1) * P], ident[:, :])
                m.then_inc(s_lp, 1)
            b = bank()
            for c in range(KT):
                m = pe.transpose(b[0:RANK, c * P:(c + 1) * P], lbsr[:, c, :], ident[:, :])
            m.then_inc(s_lp, 1)
            pe.wait_ge(s_le, 4 + 1 + 4)
            for half in range(2):
                b = bank()
                for k in range(KT):
                    m = pe.matmul(b[:, :], gsel[:, k * 256 + half * P:k * 256 + (half + 1) * P], lbT[:, k, :],
                                  start=(k == 0), stop=(k == KT - 1))
                m.then_inc(s_lp, 1)

        @block.tensor
        def _(pe):
            ring = [stp[0][:, 0, :], stp[0][:, 1, :], stp[1][:, 0, :], stp[1][:, 1, :]]
            pe.wait_ge(s_ident, 16)
            for i in range(4):
                pe.wait_ge(s_xn, i + 1)
                for t in range(4):
                    n = 4 * i + t
                    if n >= 4:
                        pe.wait_ge(s_xte, n - 3)
                    for k in range(KT):
                        m = pe.transpose(ring[n % 4][:, k * P:(k + 1) * P], xin[i % 2][:, t, k * P:(k + 1) * P], ident[:, :])
                    m.then_inc(s_xt, 1)
                if i == 1:
                    lora_prep(pe)

            qks, vs, negTs = Tally(), Tally(), Tally()
            loaded = [Tally(), Tally()]
            vloaded = Tally()
            stacked = Tally()
            maxed = Tally()
            negd = Tally()
            pairs = Tally()
            chunks = Tally()
            exps = Tally()

            held = []

            def misc_free(trip):
                if held:
                    s, tally, rate = held[-1]
                    pe.wait_ge(s, tally.back(trip, 0, rate))

            def misc_used(ins, s, tally, rate):
                ins.then_inc(s_misc, 1)
                tally.add()
                held.append((s, tally, rate))

            def qk_part(trip, ahead, c, ks_):
                u = ahead % STEPS
                g, b = u % 2, u // 2
                if ks_[0] == 0:
                    misc_free(trip)
                    if c == 0 and b == 0:
                        loaded[g].add(32)
                        pe.wait_ge(s_w[g], loaded[g].back(trip, 0, 32))
                for k in ks_:
                    m = pe.matmul(miscp[:, :], wqk[g][:, k, :],
                                  xnT[:, k, b * SEQ + c * CH:b * SEQ + (c + 1) * CH], start=(k == 0), stop=(k == KT - 1))
                if ks_[-1] == KT - 1:
                    misc_used(m, s_hi, qks, CHUNKS * STEPS)

            def v_part(trip, ahead, half):
                b = ahead % STEPS // 2
                misc_free(trip)
                if half == 0 and b == 0:
                    vloaded.add(16)
                    pe.wait_ge(s_wv, vloaded.back(trip, 0, 16))
                for t in range(4):
                    tt = b * QT + half * 4 + t
                    for k in range(KT):
                        m = pe.matmul(miscp[:, t * P:(t + 1) * P], xnT[:, k, tt * P:(tt + 1) * P], wv[:, k, :],
                                      start=(k == 0), stop=(k == KT - 1))
                misc_used(m, s_v, vs, STEPS)

            def max_part(trip, ahead, i):
                u = ahead % STEPS
                h, t, c = MAXES[i]
                if i == 0:
                    stacked.add(16 * 13)
                    pe.wait_ge(s_stack, stacked.back(trip, 0, 16 * 13 * STEPS))
                if maxed.n >= 2:
                    pe.wait_ge(s_mx_free, maxed.back(trip, 1, NM * STEPS))
                w = keys_of(t, c)
                pe.matmul(mxp[maxed.n % 2][:, 0:w], qs[u][0:ROWS_MAX, h, t * P:(t + 1) * P],
                          ks[u][0:ROWS_MAX, h, c * CH:c * CH + w], start=True, stop=True).then_inc(s_mx, 1)
                maxed.add()

            def neg_part(trip):
                misc_free(trip)
                negd.add()
                pe.wait_ge(s_neg, negd.back(trip, 0, STEPS))
                m = pe.matmul(miscp[0:PIECES * HG * QT, 0:P], negmax[:, :, :].rearrange("p a b -> p (a b)"),
                              identb[:, :], start=True, stop=True)
                misc_used(m, s_negT, negTs, STEPS)

            def score_part(trip, u, n, pair):
                c, kb = UNITS[n]
                w = width(n)
                pe.wait_ge(s_exp, pairs.back(trip, 0, 2 * NU * STEPS) + 1)
                for j in range(2):
                    h = 2 * pair + j
                    m = pe.matmul(stp[pairs.n % 2][:, j, 0:w], ks[u][0:ROWS_ALL, h, kb * P:(kb + 1) * P],
                                  qs[u][0:ROWS_ALL, h, (c + 1) * CH - w:(c + 1) * CH], start=True,
                                  stop=not diagonal(n))
                    if diagonal(n):
                        m = pe.matmul(stp[pairs.n % 2][:, j, 0:P], identb[:, :], maskb[:, :], start=False, stop=True)
                m.then_inc(s_scores, 1)
                pairs.add()

            def pv_part(trip, u, n):
                c, kb = UNITS[n]
                w = width(n)
                g, b = u % 2, u // 2
                exps.add(2)
                pe.wait_ge(s_exp, exps.back(trip, 0, 2 * NU * STEPS) + 2)
                if kb == 0:
                    chunks.add()
                    pe.wait_ge(s_acc_free, chunks.back(trip, 0, CHUNKS * STEPS))
                for h in range(HG):
                    m = pe.matmul(accp[VC * h:VC * (h + 1), CH - w:CH], va[b][:, kb, g * HG + h, :],
                                  probs[(exps.n // 2 - 1) % 3][:, h, 0:w], start=(kb == 0),
                                  stop=(n == NU - 1 or UNITS[n + 1][0] != c))
                m.then_inc(s_pv, 1)

            pe.wait_ge(s_xte, TOK // P)
            pe.wait_ge(s_le, 12)
            for ahead in range(2):
                for c in range(CHUNKS):
                    qk_part(0, ahead, c, range(KT))
                if ahead == 0:
                    v_part(0, 0, 0)
                    v_part(0, 0, 1)
            for i in range(NM):
                max_part(0, 0, i)
            pe.wait_ge(s_const, 64)
            neg_part(0)
            pe.sem_inc(s_pv, 3)

            def step(trip, u, last):
                step.n += 16
                pe.wait_ge(s_negrows, step.n if isinstance(trip, int) else trip * 16 * STEPS + step.n)
                next_max = not (last and u == 3)
                next_qk = not (last and u >= 2)
                for n in range(NU):
                    todo = list(maxes_of(n)) if next_max else []
                    for pair in range(2):
                        score_part(trip, u, n, pair)
                        if todo:
                            max_part(trip, u + 1, todo.pop(0))
                    if next_qk and n < 4:
                        qk_part(trip, u + 2, n // 2, [2 * (n % 2), 2 * (n % 2) + 1])
                    if todo:
                        max_part(trip, u + 1, todo.pop(0))
                    if n:
                        pv_part(trip, u, n - 1)
                    while todo:
                        max_part(trip, u + 1, todo.pop(0))
                    if next_qk and u % 2 == 0 and n in (8, 9):
                        v_part(trip, u + 2, n - 8)
                    if n == NU - 1:
                        if next_max:
                            neg_part(trip)
                        pv_part(trip, u, n)

            step.n = 0
            with pe.Fori(0, DTS - 1, 1) as trip:
                for u in range(STEPS):
                    step(trip, u, False)
            more = DTS - 2
            qks.n += CHUNKS * STEPS * more
            vs.n += STEPS * more
            negTs.n += STEPS * more
            for g in range(2):
                loaded[g].n += 32 * more
            vloaded.n += 16 * more
            stacked.n += 16 * 13 * STEPS * more
            maxed.n += NM * STEPS * more
            negd.n += STEPS * more
            pairs.n += 2 * NU * STEPS * more
            exps.n += 2 * NU * STEPS * more
            chunks.n += CHUNKS * STEPS * more
            step.n += 16 * STEPS * more
            for u in range(STEPS):
                step(DTS - 1, u, True)

            pe.wait_ge(s_f0, 32)
            fring = [mxp[0], mxp[1], miscp]
            oring = [stp[0][:, 0, :], stp[0][:, 1, :], stp[1][:, 0, :], stp[1][:, 1, :]]
            pe.wait_ge(s_exp, 2 + pairs.n)
            pe.wait_ge(s_mx_free, maxed.n)
            pe.wait_ge(s_negT, negTs.n)
            for i in range(4):
                for j in range(2):
                    g = 2 * i + j
                    for k in range(KT):
                        m = pe.matmul(oring[i][0:RC, j * GTOK:(j + 1) * GTOK], acat2[:, k, g * RC:(g + 1) * RC],
                                      xnT[:, k, g * GTOK:(g + 1) * GTOK], start=(k == 0), stop=(k == KT - 1))
                m.then_inc(s_ax, 1)
            pe.wait_ge(s_bc, 32)
            pe.wait_ge(s_axe, 4)

            def ffn(i):
                g = i * P // GTOK
                if i >= 3:
                    pe.wait_ge(s_z, i - 2)
                for k in range(KT):
                    pe.matmul(fring[i % 3][:, :], xnT[:, k, i * P:(i + 1) * P], wf[:, k, :], start=(k == 0), stop=False)
                pe.matmul(fring[i % 3][:, :], axT[0:RC, i * P:(i + 1) * P], bcat2[g // 4][:, g % 4, :],
                          start=False, stop=True).then_inc(s_ff, 1)

            def project(i):
                if i == 0:
                    pe.wait_ge(s_wp, 16)
                    pe.wait_ge(s_att, DTS)
                if i >= 4:
                    pe.wait_ge(s_y, i - 3)
                for k in range(KT):
                    m = pe.matmul(oring[i % 4], att[:, k, i * P:(i + 1) * P], wp[:, k, :], start=(k == 0), stop=(k == KT - 1))
                m.then_inc(s_op, 1)

            LAGF = 4
            for i in range(TOK // P + LAGF):
                if i < TOK // P:
                    ffn(i)
                if i >= LAGF:
                    project(i - LAGF)

        @block.scalar
        def _(act):
            ring = [stp[0][:, 0, :], stp[0][:, 1, :], stp[1][:, 0, :], stp[1][:, 1, :]]
            for i in range(4):
                act.wait_ge(s_var, i + 1)
                act.activation(std[:, :], meanvar[:, :, 1], ACT.Sqrt).then_inc(s_std, 1)
                for t in range(4):
                    n = 4 * i + t
                    act.wait_ge(s_xt, n + 1)
                    act.activation(xnT[:, :, n * P:(n + 1) * P], ring[n % 4].rearrange("p (k m) -> p k m", k=KT),
                                   ACT.Copy).then_inc(s_xte, 1)

            miscs = Tally()
            stacked = Tally()
            pairs = Tally()
            used = Tally()
            negs = Tally()
            RM = 3 * STEPS + 4

            def misc_full(trip):
                miscs.add()
                act.wait_ge(s_misc, miscs.back(trip, 0, RM))

            def qk_out(trip, ahead, c):
                g = ahead % 2
                if c == 0 and stacked.n:
                    act.wait_ge(s_stack, stacked.back(trip, 0, 16 * 13 * STEPS))
                misc_full(trip)
                part = slice(c * CH, (c + 1) * CH)
                act.activation(qk[:, part], miscp[:, :], ACT.Identity, bias=bqk[g][:, 0:1])
                act.activation(pieces[:, 0, part], miscp[:, :], ACT.Identity, bias=bqk[g][:, 0:1])\
                   .then_inc(s_hi, 1)
                if c == 1:
                    stacked.add(16 * 13)

            def v_out(trip, ahead, half):
                b = ahead % STEPS // 2
                misc_full(trip)
                act.activation(va[b][:, half * 4:(half + 1) * 4, :, :].rearrange("p t h (d e) -> p (t h d) e", e=2)[:, :, 0],
                               miscp[:, :], ACT.Copy).then_inc(s_v, 1)

            def neg_out(trip):
                misc_full(trip)
                if negs.n:
                    act.wait_ge(s_negrows, negs.back(trip, 0, 16 * STEPS))
                act.activation(negmaxT[:, :], miscp[0:PIECES * HG * QT, 0:P], ACT.Copy)\
                   .then_inc(s_negT, 1)
                negs.add(16)

            for ahead in range(2):
                for c in range(CHUNKS):
                    qk_out(0, ahead, c)
                if ahead == 0:
                    v_out(0, 0, 0)
                    v_out(0, 0, 1)
            neg_out(0)
            act.sem_inc(s_exp, 2)

            def step(trip, u, last):
                next_max = not (last and u == 3)
                next_qk = not (last and u >= 2)
                for n in range(NU):
                    w = width(n)
                    buf = probs[used.n % 3]
                    act.wait_ge(s_pv, used.back(trip, 0, NU * STEPS) + 1)
                    for pair in range(2):
                        i = pairs.n
                        pairs.add()
                        act.wait_ge(s_scores, pairs.back(trip, 0, 2 * NU * STEPS))
                        act.activation(buf[:, 2 * pair:2 * pair + 2, 0:w], stp[i % 2][:, :, 0:w], ACT.Exp,
                                       scale=SCALE).then_inc(s_exp, 1)
                    used.add()
                    if next_qk and n in (1, 3):
                        qk_out(trip, u + 2, n // 2)
                    if next_qk and u % 2 == 0 and n in (8, 9):
                        v_out(trip, u + 2, n - 8)
                    if next_max and n == NU - 1:
                        neg_out(trip)

            with act.Fori(0, DTS - 1, 1) as trip:
                for u in range(STEPS):
                    step(trip, u, False)
            more = DTS - 2
            miscs.n += RM * more
            stacked.n += 16 * 13 * STEPS * more
            pairs.n += 2 * NU * STEPS * more
            used.n += NU * STEPS * more
            negs.n += 16 * STEPS * more
            for u in range(STEPS):
                step(DTS - 1, u, True)

            oring = [stp[0][:, 0, :], stp[0][:, 1, :], stp[1][:, 0, :], stp[1][:, 1, :]]
            act.wait_ge(s_pv, 3 + NU * STEPS * DTS)
            for i in range(4):
                act.wait_ge(s_ax, i + 1)
                act.activation(axT[0:RC, i * CH:(i + 1) * CH], oring[i][0:RC, :], ACT.Copy).then_inc(s_axe, 1)
            act.wait_ge(s_pv, 3 + NU * STEPS * DTS)
            for i in range(TOK // P):
                act.wait_ge(s_z, i + 1)
                if i >= NG:
                    act.wait_ge(s_yg, i - NG + 1)
                act.activation(g_t[i % NG], z_t[i % 2], ACT.Silu).then_inc(s_g, 1)

        def lora_vec(dve):
            uses = [0]
            banks = [mxp[0], mxp[1], accp, miscp]

            def bank():
                n = uses[0]
                uses[0] += 1
                dve.wait_ge(s_lp, n + 1)
                return banks[n % 4]

            dve.wait_ge(s_lora, 16 * 9)
            for n in range(LORAS):
                k, p0 = n // 4, (n % 4) * RANK
                m = dve.tensor_copy(gatep[p0:p0 + RANK, k * GROUPS:(k + 1) * GROUPS],
                                    gateall[p0:p0 + RANK, n:GROUPS * LORAS:LORAS])
            m.then_inc(s_gsel, 1)
            dve.wait_ge(s_gsel, 1)
            for k in range(KT):
                for b in range(GROUPS):
                    o = k * 256 + b * RANK
                    m = dve.tensor_scalar(gsel[:, o:o + RANK], pick, gatep[:, k * GROUPS + b:k * GROUPS + b + 1], None, ALU.mult)
            m.then_inc(s_gsel, 1)
            for it in range(KT):
                dve.tensor_copy(acat[:, it, :, 0:RANK], bank()[:, 0:256].rearrange("p (g r) -> p g r", g=GROUPS))\
                   .then_inc(s_le, 1)
            b = bank()
            for g in range(GROUPS):
                m = dve.tensor_copy(acat[:, :, g, RANK:RC], b[:, 0:KT * RANK].rearrange("p (k r) -> p k r", k=KT))
            m.then_inc(s_le, 1)
            for k in range(KT):
                dve.tensor_copy(lbT[:, k, :], bank()[:, :]).then_inc(s_le, 1)
            dve.tensor_copy(lbsT, bank()[0:RANK, :]).then_inc(s_le, 1)
            for half in range(2):
                dve.tensor_copy(beff[:, half, :], bank()[:, :]).then_inc(s_le, 1)

        @block.vector
        def _(dve):
            for i in range(4):
                dve.wait_ge(s_x[i], 16)
                for t in range(4):
                    dve.bn_stats(stats[:, t, :], xin[i % 2][:, t, :]).then_inc(s_stats, 1)
                dve.wait_ge(s_stats, 5 * i + 4)
                for t in range(4):
                    m = dve.bn_aggr(meanvar[:, t, :], stats[:, t, :])
                m.then_inc(s_stats, 1)
                dve.wait_ge(s_stats, 5 * i + 5)
                dve.tensor_scalar(meanvar[:, :, 1], meanvar[:, :, 1], EPS, None, ALU.add).then_inc(s_var, 1)
                dve.wait_ge(s_std, i + 1)
                dve.reciprocal(rstd[:, :], std[:, :]).then_inc(s_rstd, 1)
                dve.wait_ge(s_rstd, i + 1)
                for t in range(4):
                    m = dve.tensor_scalar(xin[i % 2][:, t, :], xin[i % 2][:, t, :], meanvar[:, t, 0:1], rstd[:, t:t + 1],
                                          ALU.subtract, ALU.mult)
                m.then_inc(s_xn, 1)
                if i == 0:
                    for b in range(BATCH):
                        dve.memset(va[b][:, :, :, :].rearrange("p t h (d e) -> p (t h d) e", e=2)[:, :, 1], 1.0)
                    dve.memset(tops[:, :, :], NEG)
                if i == 1:
                    lora_vec(dve)
            dve.wait_ge(s_lst, 16 * (1 + 2 * GROUPS))
            for i in range(STEPS):
                dve.memset(qs[i][ALIBI0:ROWS_ALL, :, :], 1.0)
                m = dve.memset(ks[i][ALIBI0:ROWS_ALL, :, :], 1.0)
            m.then_inc(s_init, 1)

            maxed = Tally()
            links = Tally()
            negs = Tally()
            miscs = Tally()
            accs = Tally()
            pvs = Tally()
            rawd = Tally()

            def max_part(trip, i):
                h, t, c = MAXES[i]
                w = keys_of(t, c)
                bank = mxp[maxed.n % 2]
                maxed.add()
                dve.wait_ge(s_mx, maxed.back(trip, 0, NM * STEPS))
                to = tops[:, c, h * QT + t:h * QT + t + 1]
                if t // CT == c:
                    dve.sem_inc(s_seen, 1)
                    m = dve.tensor_tensor_reduce(junk[:, (maxed.n - 1) % 2, 0:w], bank[:, 0:w], mask[:, CH - w:CH],
                                                 1.0, NEG, ALU.add, ALU.max, to)
                else:
                    m = dve.tensor_reduce(to, bank[:, 0:w], AX.X, ALU.max)
                m.then_inc(s_mx_free, 1)

            def neg_part(trip):
                dve.wait_ge(s_mx_free, maxed.back(trip, 0, NM * STEPS))
                if negs.n:
                    dve.wait_ge(s_negT, negs.back(trip, 0, STEPS))
                negs.add()

                def link(ins):
                    ins.then_inc(s_top, 1)
                    links.add()
                    dve.wait_ge(s_top, links.back(trip, 0, 4 * STEPS))

                link(dve.tensor_tensor(top[:, :], tops[:, 0, :], tops[:, 1, :], ALU.max))
                link(dve.tensor_scalar(negmax[:, 0, :], top[:, :], -1.0, None, ALU.mult))
                link(dve.scalar_tensor_tensor(out=toprest[:, :], in0=top[:, :], scalar=-1.0, in1=negmax[:, 0, :],
                                              op0=ALU.mult, op1=ALU.subtract))
                link(dve.tensor_copy(negmax[:, 1, :], toprest[:, :]))
                dve.tensor_tensor(negmax[:, 2, :], toprest[:, :], negmax[:, 1, :], ALU.subtract).then_inc(s_neg, 1)

            def acc_out(trip, c):
                pvs.add(CT * (c + 1))
                dve.wait_ge(s_pv, pvs.back(trip, 0, NU * STEPS) + 3)
                if c == 0:
                    rawd.add(32)
                dve.wait_ge(s_raw[c], rawd.back(trip, 0, 32 * STEPS))
                dve.tensor_copy(raw[c][:, :], accp[:, :]).then_inc(s_acc_free, 1)

            dve.wait_ge(s_const, 64)
            for i in range(NM):
                max_part(0, i)
            neg_part(0)
            dve.sem_inc(s_acc_free, 1)

            def step(trip, u, last):
                next_max = not (last and u == 3)
                for n in range(NU):
                    if next_max:
                        for i in maxes_of(n):
                            max_part(trip, i)
                    if n == CT:
                        acc_out(trip, 0)
                    if next_max and n == NU - 2:
                        neg_part(trip)
                acc_out(trip, 1)

            with dve.Fori(0, DTS - 1, 1) as trip:
                for u in range(STEPS):
                    step(trip, u, False)
            more = DTS - 2
            maxed.n += NM * STEPS * more
            links.n += 4 * STEPS * more
            negs.n += STEPS * more
            pvs.n += NU * STEPS * more
            rawd.n += 32 * STEPS * more
            for u in range(STEPS):
                step(DTS - 1, u, True)

            dve.wait_ge(s_sums, 16)
            dve.reciprocal(inv, sums).then_inc(s_inv, 1)
            for c in range(CHUNKS):
                dve.wait_ge(s_raw[c], 32 * (1 + STEPS * DTS))
            for dt in range(DTS):
                dve.wait_ge(s_invb[dt % 2], 16 * (dt // 2 + 1))
                dve.tensor_tensor(att[:, dt, :], att[:, dt, :], invb[dt % 2], ALU.mult).then_inc(s_am, 1)
                dve.wait_ge(s_am, dt + 1)
                dve.tensor_scalar(att[:, dt, :], att[:, dt, :], bv[:, dt:dt + 1], None, ALU.add).then_inc(s_att, 1)
            fring = [mxp[0], mxp[1], miscp]
            oring = [stp[0][:, 0, :], stp[0][:, 1, :], stp[1][:, 0, :], stp[1][:, 1, :]]
            dve.wait_ge(s_fb, 32)
            for i in range(TOK // P + 4):
                if i < TOK // P:
                    dve.wait_ge(s_ff, i + 1)
                    if i >= 2:
                        dve.wait_ge(s_g, i - 1)
                    dve.tensor_tensor(z_t[i % 2], fring[i % 3][:, :], bfb[:, :], ALU.add).then_inc(s_z, 1)
                j = i - 4
                if j >= 0:
                    dve.wait_ge(s_op, j + 1)
                    if j >= 2:
                        dve.wait_ge(s_out[j % 2], 16 * (j // 2))
                    dve.tensor_tensor(y_t[j % 2], oring[j % 4], bpb[:, :], ALU.add).then_inc(s_y, 1)

        @block.gpsimd
        def _(pool):
            hi = Tally()
            mids = Tally()
            rests = Tally()

            def split(trip, ahead):
                hi.add(CHUNKS)
                pool.wait_ge(s_hi, hi.back(trip, 0, CHUNKS * STEPS))
                pool.tensor_tensor(pieces[:, 1, :], qk[:, :], pieces[:, 0, :], ALU.subtract).then_inc(s_mid, 1)
                mids.add()
                pool.wait_ge(s_mid, mids.back(trip, 0, STEPS))
                pool.tensor_tensor(qk[:, :], qk[:, :], pieces[:, 0, :], ALU.subtract).then_inc(s_rest, 1)
                rests.add()
                pool.wait_ge(s_rest, rests.back(trip, 0, STEPS))
                pool.tensor_tensor(pieces[:, 2, :], qk[:, :], pieces[:, 1, :], ALU.subtract).then_inc(s_lo, 1)

            split(0, 0)
            split(0, 1)

            def step(trip, u, last):
                if not (last and u >= 2):
                    split(trip, u + 2)

            with pool.Fori(0, DTS - 1, 1) as trip:
                for u in range(STEPS):
                    step(trip, u, False)
            more = DTS - 2
            hi.n += CHUNKS * STEPS * more
            mids.n += STEPS * more
            rests.n += STEPS * more
            for u in range(STEPS):
                step(DTS - 1, u, True)

            for i in range(TOK // P):
                y = y_t[i % 2]
                pool.wait_ge(s_y, i + 1)
                pool.wait_ge(s_g, i + 1)
                pool.tensor_tensor(y, y, g_t[i % NG], ALU.mult).then_inc(s_yg, 1)
                pool.wait_ge(s_yg, i + 1)
                b = i // 4 % 3
                pool.wait_ge(s_xl[b], 16 * (i // 12 + 1))
                pool.tensor_tensor(y, y, xt[b][:, i % 4, :], ALU.add).then_inc(s_res, 1)


_INS = ["L0_attn_hidden_states", "L0_attn_w_attn", "L0_attn_b_attn", "L0_attn_w_proj", "L0_attn_b_proj",
        "L0_ffn_gate", "L0_ffn_kernel", "L0_ffn_bias", "L0_ffn_lora_A", "L0_ffn_lora_B",
        "L0_ffn_lora_A_shared", "L0_ffn_lora_B_shared"]


def _constants():
    import numpy as np

    bf = np.dtype("bfloat16")
    ident = np.eye(P, dtype=np.float32)
    mask = np.zeros((P, CH), np.float32)
    mask[:, CH - P:] = np.where(np.arange(P)[None, :] > np.arange(P)[:, None], np.float32(NEG), np.float32(0))
    maskb = np.where(np.arange(P)[:, None] > np.arange(P)[None, :], np.float32(-1e30), np.float32(0)).astype(bf)
    slopes = (np.float32(2 ** (-2 ** (-(5 - 3)))) ** np.arange(1, HEADS + 1, dtype=np.float32)).astype(np.float32)
    term = (slopes[:, None] * np.arange(SEQ, dtype=np.float32)[None, :] / np.float32(SCALE)).astype(np.float32)
    parts = []
    for _ in range(PIECES):
        part = term.astype(bf)
        parts.append(part)
        term = term - part.astype(np.float32)
    alibi = np.stack(parts, 1).reshape(HEADS // HG, HG, PIECES, SEQ).transpose(0, 2, 1, 3)
    pick = np.tile(np.eye(RANK, dtype=np.float32), (P // RANK, 1))
    return {"c_ident": ident, "c_identb": ident.astype(bf), "c_mask": mask, "c_maskb": maskb,
            "c_alibi": np.ascontiguousarray(alibi.reshape(HEADS // HG, PIECES, HG * SEQ)), "c_pick": pick}


def _by_group(w, b):
    import numpy as np

    w = w.reshape(HID, 3, HEADS // HG, HG, HD)
    b = b.reshape(3, HEADS // HG, HG, HD)
    return {"w_qk": np.ascontiguousarray(w[:, :2].transpose(2, 0, 1, 4, 3).reshape(HEADS // HG, HID, P)),
            "b_qk": np.ascontiguousarray(b[:2].transpose(1, 0, 3, 2).reshape(HEADS // HG, P)),
            "w_v": np.ascontiguousarray(w[:, 2].reshape(HID, HID)),
            "b_v": np.ascontiguousarray(b[2].reshape(KT, P).T)}


def kernel(**inputs):
    import numpy as np
    import concourse.bacc as bacc
    from concourse.bass_utils import run_bass_kernel_spmd

    nc = bacc.Bacc("TRN2", target_bir_lowering=False, num_devices=1)
    arrays = {f"in_{name}": np.ascontiguousarray(inputs[name]) for name in _INS if "_attn_w_attn" not in name
              and "_attn_b_attn" not in name}
    arrays.update(_by_group(np.asarray(inputs["L0_attn_w_attn"]), np.asarray(inputs["L0_attn_b_attn"])))
    arrays.update(_constants())
    args = {name: nc.dram_tensor(name, a.shape, mybir.dt.from_np(a.dtype), kind="ExternalInput").ap()
            for name, a in arrays.items()}
    out = nc.dram_tensor("out", [TOK, HID], F32, kind="ExternalOutput").ap()
    flat = args["in_L0_attn_hidden_states"].rearrange("b s d -> (b s) d")
    rest = [args[f"in_{name}"] for name in _INS[3:]]
    attention_and_gate(nc, flat, args["w_qk"], args["w_v"], args["b_qk"], args["b_v"], *rest, args["c_ident"], args["c_identb"], args["c_mask"], args["c_maskb"], args["c_alibi"],
                       args["c_pick"], out)
    got = run_bass_kernel_spmd(nc, [arrays], core_ids=[0])
    return got.results[0]["out"].reshape(BATCH, SEQ, HID)
```

```python
from contextlib import ExitStack

import concourse.bass as bass
from concourse import mybir

F32 = mybir.dt.float32
BF16 = mybir.dt.bfloat16
F16 = mybir.dt.float16
I32 = mybir.dt.int32
ALU = mybir.AluOpType
AX = mybir.AxisListType
ACT = mybir.ActivationFunctionType

P = 128
BATCH, SEQ, HID = 2, 1024, 512
TOK = BATCH * SEQ
HEADS = 32
HD = HID // HEADS
KT = HID // P
HG = 4
DT_HEADS = P // HD
DTS = HEADS // DT_HEADS
STEPS = 4
CH = 512
CHUNKS = SEQ // CH
QT = SEQ // P
CT = CH // P
PIECES = 3
PROD = 6 * HD
ALIBI0 = PROD
NEGMAX0 = PROD + PIECES
ROWS_MAX = NEGMAX0
ROWS_ALL = NEGMAX0 + PIECES
Q_PIECES = [0, 0, 0, 1, 1, 2]
K_PIECES = [0, 1, 2, 0, 1, 0]
SCALE = 1.0 / HD
NEG = -3.0e38
EPS = 1e-5
HALVES = 2
PASSES = [(0, 0), (0, 1), (1, 0)]
X_SCALE = 2.0 ** 11
W_SCALE = 2.0 ** 14
EXPONENT = 0x7F800000
SMALLEST = 1e-18
VC = 2 * HD

LORAS, RANK, GROUPS = 16, 32, 8
GTOK = TOK // GROUPS
NR = LORAS * RANK
RC = 2 * RANK

UNITS = [(c, kb) for c in range(CHUNKS) for kb in range(CT * (c + 1))]
NU = len(UNITS)
ITEMS = sorted(((t, c) for t in range(QT) for c in range(t // CT + 1)),
               key=lambda item: min(CH, (item[0] + 1) * P - item[1] * CH))
PER_UNIT = HG * len(ITEMS) // NU
SHARE = len(ITEMS) // PER_UNIT
MAXES = [(h, *item) for h in range(HG) for i in range(SHARE)
         for item in (ITEMS[i], *ITEMS[2 * SHARE + 2 * i:2 * SHARE + 2 * i + 2], ITEMS[2 * SHARE - 1 - i])]
NM = len(MAXES)
HALF_U, HALF_M = NU // 2, NM // 2
PER_FFN = 5
FIRST_MAXES = [(0, i) for i in range(NM)] + [(1, i) for i in range(HALF_M)]
LINKS = 5
NT = TOK // P
QK_AT = (3, 7)
NEG_AT = -(-NM // PER_FFN)


FILL = {0: [("qk", 0, 0)], 1: [("qk", 0, 1)], 2: [("qk", 0, 2), ("qk", 0, 3)],
        3: [("qk", 1, 0)], 4: [("qk", 1, 1)], 5: [("qk", 1, 2)], 6: [("qk", 1, 3)],
        7: [("neg",)], 8: [("v", 0)], 9: [("v", 1)], 10: [("v", 2), ("v", 3)]}
LATE = (3, 7, 8)
WEIGHTS_AT = 2
EMPTY = {3: ("qk", 0), 7: ("qk", 1), 8: ("neg",), 11: ("v",)}


def width(n):
    c, kb = UNITS[n]
    return CH - max(0, kb - CT * c) * P


def diagonal(n):
    c, kb = UNITS[n]
    return kb >= CT * c


def maxes_of(n, near, far):
    if n < HALF_U:
        return [(1, HALF_M + PER_UNIT * n + i) for i in range(PER_UNIT)] if near else []
    return [(2, PER_UNIT * (n - HALF_U) + i) for i in range(PER_UNIT)] if far else []


def keys_of(t, c):
    return min(CH, (t + 1) * P - c * CH)


class Plan:

    def __init__(self, u, last):
        after = STEPS - 1 - u if last else STEPS
        self.near, self.far = after >= 1, after >= 2
        self.qk = after >= 3
        self.v = after >= 2
        self.neg = after >= 1


class Tally:

    def __init__(self, n=0):
        self.n = n

    def add(self, k=1):
        self.n += k
        return self.n

    def at(self, trip, rate, less=0):
        v = self.n - less
        return v if isinstance(trip, int) else trip * rate + v


def attention_and_gate(nc, x, w_qk, w_v, b_qk, b_v, w_proj, b_proj, gate, w_ffn, b_ffn, lora_a, lora_b,
                       lora_as, lora_bs, ident_d, ident16_d, identb_d, mask_d, maskb_d, alibi_d, pick_d, ones_d, out):
    ctx = ExitStack()
    with ctx:
        def sb(name, shape, dt):
            return ctx.enter_context(nc.sbuf_tensor(name, shape, dt))

        def sem(name):
            return ctx.enter_context(nc.semaphore(name))

        sums_d = nc.dram_tensor("sums_d", [HEADS, TOK], F32, kind="Internal").ap()
        inv_d = nc.dram_tensor("inv_d", [HEADS, TOK], F32, kind="Internal").ap()
        g_d = nc.dram_tensor("g_d", [TOK, HID], F32, kind="Internal").ap()

        xs = sb("xs", [P, HALVES, KT, TOK], F16)
        att = sb("att", [P, KT, TOK], F32)
        qs = [sb(f"qs{i}", [P, HG, SEQ], BF16) for i in range(STEPS)]
        ks = [sb(f"ks{i}", [P, HG, SEQ], BF16) for i in range(STEPS)]
        va = [sb(f"va{b}", [P, QT, DT_HEADS, VC], F32) for b in range(BATCH)]
        probs = [sb(f"probs{i}", [P, HG, CH], F32) for i in range(3)]
        wqk = [sb(f"wqk{g}", [P, KT, P], F32) for g in range(2)]
        wv = sb("wv", [P, KT, P], F32)
        wqks = [sb(f"wqks{g}", [P, HALVES, KT, P], F16) for g in range(2)]
        wvs = sb("wvs", [P, HALVES, KT, P], F16)
        largest = sb("largest", [P, 8], F32)
        onesf = sb("onesf", [8, P], F32)
        diag = sb("diag", [8, 8], F32)
        bound = sb("bound", [P, 3], F32)
        power = sb("power", [P, 3], F32)
        inverse_p = sb("inverse_p", [P, 3], F32)
        scale = sb("scale", [P, 3], F32)
        back = sb("back", [P, 3], F32)
        ratio = sb("ratio", [P, 1], F32)
        ident16 = sb("ident16", [P, P], F16)
        bqk = [sb(f"bqk{g}", [P, 1], F32) for g in range(2)]
        qk = sb("qk", [P, SEQ], F32)
        pieces = sb("pieces", [P, PIECES, SEQ], BF16)
        raw = [sb(f"raw{c}", [P, CH], F32) for c in range(CHUNKS)]
        mask = sb("mask", [P, CH], F32)
        maskb = sb("maskb", [P, P], BF16)
        ident = sb("ident", [P, P], F32)
        identb = sb("identb", [P, P], BF16)
        junk = sb("junk", [P, 2, CH], BF16)
        tops = sb("tops", [P, CHUNKS, HG * QT], F32)
        top = sb("top", [P, HG * QT], F32)
        toprest = sb("toprest", [P, HG * QT], F32)
        negmax = sb("negmax", [P, PIECES, HG * QT], BF16)
        negmaxT = sb("negmaxT", [PIECES * HG * QT, P], BF16)
        bv = sb("bv", [P, KT], F32)
        stats = sb("stats", [P, 4, 6], F32)
        meanvar = sb("meanvar", [P, 4, 2], F32)
        std = sb("std", [P, 4], F32)
        rstd = sb("rstd", [P, 4], F32)
        small = sb("small", [P, 352], F32)
        bfb = sb("bfb", [P, HID], F32)

        def pb(name, shape):
            return ctx.enter_context(nc.psum_tensor(name, shape, F32))

        mxp = [pb(f"mxp{i}", [P, CH]) for i in range(2)]
        stp = [pb(f"stp{i}", [P, 2, CH]) for i in range(2)]
        accp = pb("accp", [P, CH])
        miscp = pb("miscp", [P, CH])
        ring = [stp[0][:, 0, :], stp[0][:, 1, :], stp[1][:, 0, :], stp[1][:, 1, :]]

        s_ident = sem("s_ident")
        s_const = sem("s_const")
        s_ones = sem("s_ones")
        s_x = [sem(f"s_x{i}") for i in range(5)]
        s_stats = sem("s_stats")
        s_var = sem("s_var")
        s_std = sem("s_std")
        s_rstd = sem("s_rstd")
        s_xn = sem("s_xn")
        s_xhi = sem("s_xhi")
        s_xlo = sem("s_xlo")
        s_watt = sem("s_watt")
        s_large = sem("s_large")
        s_col = sem("s_col")
        s_row = sem("s_row")
        s_scale = sem("s_scale")
        s_wscaled = sem("s_wscaled")
        s_whi = sem("s_whi")
        s_wlo = sem("s_wlo")
        s_xt = sem("s_xt")
        s_xte = sem("s_xte")
        s_lora = sem("s_lora")
        s_gsel = sem("s_gsel")
        s_lp = sem("s_lp")
        s_le = sem("s_le")
        s_bcat = sem("s_bcat")
        s_wf = sem("s_wf")
        s_ax = sem("s_ax")
        s_axe = sem("s_axe")
        s_ff = sem("s_ff")
        s_z = sem("s_z")
        s_g = sem("s_g")
        s_gst = [sem(f"s_gst{i}") for i in range(2)]
        s_w = [sem(f"s_w{g}") for g in range(2)]
        s_wv = sem("s_wv")
        s_misc = sem("s_misc")
        s_hi = sem("s_hi")
        s_v = sem("s_v")
        s_mid = sem("s_mid")
        s_rest = sem("s_rest")
        s_lo = sem("s_lo")
        s_stack = sem("s_stack")
        s_mx = sem("s_mx")
        s_mx_free = sem("s_mx_free")
        s_seen = sem("s_seen")
        s_top = sem("s_top")
        s_neg = sem("s_neg")
        s_negT = sem("s_negT")
        s_negrows = sem("s_negrows")
        s_scores = sem("s_scores")
        s_exp = sem("s_exp")
        s_pv = sem("s_pv")
        s_acc_free = sem("s_acc_free")
        s_raw = [sem(f"s_raw{c}") for c in range(CHUNKS)]
        s_sums = sem("s_sums")
        s_inv = sem("s_inv")
        s_invst = sem("s_invst")
        s_invb = [sem(f"s_invb{b}") for b in range(BATCH)]
        s_am = sem("s_am")
        s_att = sem("s_att")
        s_wp = sem("s_wp")
        s_bp = sem("s_bp")
        s_xg = [sem(f"s_xg{i}") for i in range(4)]
        s_op = sem("s_op")
        s_y = sem("s_y")
        s_yg = sem("s_yg")
        s_res = sem("s_res")
        s_out = sem("s_out")

        def f32view(t):
            return t[:, :, :].rearrange("p a b -> p (a b)").bitcast(F32)

        xin = [*probs, va[1][:, :, :, :].rearrange("p a b c -> p (a b c)").rearrange("p (t d) -> p t d", t=4)]
        la = f32view(qs[1]).rearrange("p (k i) -> p k i", k=KT)
        lbr = f32view(ks[1]).rearrange("p (c m) -> p c m", c=KT)
        lbT = att[:, 2, :].rearrange("p (c m) -> p c m", c=KT)
        acat = att[:, 3, :].bitcast(F16).rearrange("p (a k g r) -> p a k g r", a=HALVES, k=KT, g=GROUPS)
        wfs = att[:, 1, :].bitcast(F16).rearrange("p (a k o) -> p a k o", a=HALVES, k=KT)
        watt = att[:, 0:3, :].rearrange("p a n -> p (a n)")
        xp = [t[:, :, :].rearrange("p a b -> p (a b)").bitcast(F16).rearrange("p (a t d) -> p a t d", a=HALVES, t=4)
              for t in (qs[2], qs[3], ks[2], ks[3])]
        axT = att[:, 0, :]
        va1 = va[1][:, :, :, :].rearrange("p a b c -> p (a b c)")
        gsel = va1[:, 0:KT * GROUPS * RANK]
        beff = va1[:, 1024:1024 + 2 * HID].rearrange("p (a o) -> p a o", a=2)
        bcat = [f32view(t)[0:RC, :].rearrange("p (g o) -> p g o", g=4) for t in (qs[3], ks[3])]
        wf = probs[0]
        las = raw[0][0:RANK, :]
        lbsT = raw[1][0:RANK, :]
        lbsr = small[:, 0:128].rearrange("p (c r) -> p c r", c=KT)
        pick = small[:, 128:160]
        gatep = small[:, 160:192]
        gateall = small[:, 192:320]
        z_t = raw
        g_t = [probs[1 + i // 4][:, i % 4, :] for i in range(8)]

        invb = [[f32view(t)[:, j * SEQ:(j + 1) * SEQ] for t in pair for j in range(2)]
                for pair in ((qs[0], ks[0]), (qs[1], ks[1]))]
        wp = f32view(qs[2]).rearrange("p (k o) -> p k o", k=KT)
        va_t = [t[:, :, :, :].rearrange("p a b c -> p (a b c)").rearrange("p (t d) -> p t d", t=4) for t in va]
        xt = [f32view(ks[2]).rearrange("p (t d) -> p t d", t=4), probs[0], probs[1], probs[2]]
        gt = [va_t[0], va_t[1], f32view(ks[3]).rearrange("p (t d) -> p t d", t=4), xs[:, 0, 0:2, :].rearrange("p k n -> p (k n)").bitcast(F32).rearrange("p (t d) -> p t d", t=4)]
        y_t = [f32view(qs[3]).rearrange("p (t d) -> p t d", t=4)[:, i, :] for i in range(4)]
        sums = [qk[:, b * 256:(b + 1) * 256] for b in range(BATCH)]
        inv = [qk[:, 512 + b * 256:512 + (b + 1) * 256] for b in range(BATCH)]

        block = ctx.enter_context(nc.Block())

        def dt_of(trip, ahead):
            return trip + ahead // STEPS

        def repeated(a, at, n):
            return bass.AP(tensor=a.tensor, offset=a.offset, ap=[*a.ap[:at], [0, n], *a.ap[at:]])

        def row(a):
            return bass.AP(tensor=a.tensor, offset=a.offset, ap=[[0, P], [1, HID]])

        @block.sync
        def _(sp):
            def load_x(i, lo, hi, sem):
                sp.dma_start(xin[i][:, lo:hi, :],
                             x[(4 * i + lo) * P:(4 * i + hi) * P, :].rearrange("(t p) d -> p t d", p=P)).then_inc(sem, 16)

            def load_wqk(g, dt):
                sp.dma_start(wqk[g][:, :, :], w_qk[bass.ds(dt * 2 + g, 1)].rearrange("g (k p) n -> p (g k) n", p=P))\
                  .then_inc(s_w[g], 16)
                sp.dma_start(bqk[g][:, :], b_qk[bass.ds(dt * 2 + g, 1)].rearrange("g p -> p g"),
                             allow_slow_non_contiguous=True).then_inc(s_w[g], 16)

            def load_wv(dt):
                sp.dma_start(wv[:, :, :], w_v.rearrange("(k p) n -> p k n", p=P)[:, :, bass.ds(dt * P, P)])\
                  .then_inc(s_wv, 16)

            load_x(0, 0, 2, s_x[0])
            load_x(0, 2, 4, s_x[4])
            sp.dma_start(ident[:, :], ident_d).then_inc(s_ident, 16)
            sp.dma_start(ident16[:, :], ident16_d).then_inc(s_ident, 16)
            load_x(1, 0, 4, s_x[1])
            sp.dma_start(watt[:, 0:4 * SEQ].rearrange("p (g k n) -> p g k n", g=2 * DTS, k=KT)
                         .rearrange("p g k n -> p (g k) n"),
                         w_qk.rearrange("g (k p) n -> p (g k) n", p=P)).then_inc(s_watt, 16)
            sp.dma_start(watt[:, 4 * SEQ:6 * SEQ].rearrange("p (k n) -> p k n", k=KT),
                         w_v.rearrange("(k p) n -> p k n", p=P)).then_inc(s_watt, 16)
            load_wqk(0, 0)
            load_wv(0)
            load_x(2, 0, 4, s_x[2])
            load_x(3, 0, 4, s_x[3])
            load_wqk(1, 0)
            for tile, src in ((pick, pick_d), (gateall, bass.AP(tensor=gate.tensor, offset=gate.offset,
                                                                ap=[[0, P], [1, GROUPS * LORAS]])),
                              (la, lora_a.rearrange("n r i -> (n r) i").rearrange("(k p) i -> p k i", p=P)),
                              (las[:, :], lora_as), (lbsr, lora_bs.rearrange("(c p) r -> p c r", p=P))):
                sp.dma_start(tile, src).then_inc(s_lora, 16)
            for c in range(KT):
                sp.dma_start(lbr.rearrange("p c (n r) -> p c n r", r=RANK)[:, c],
                             lora_b[:, c * P:(c + 1) * P, :].rearrange("n o r -> o n r")).then_inc(s_lora, 16)
            for t in (qs[0], ks[0]):
                sp.dma_start(t[ALIBI0:ROWS_ALL, :, :], ones_d).then_inc(s_ones, 16)
            sp.wait_ge(s_xlo, 4)
            sp.dma_start(wf[:, :, :], w_ffn.rearrange("(k p) o -> p k o", p=P)).then_inc(s_wf, 16)
            sp.dma_start(bfb[:, :], row(b_ffn)).then_inc(s_wf, 16)
            for tile, src in ((identb, identb_d), (mask, mask_d), (maskb, maskb_d), (bv, b_v)):
                sp.dma_start(tile[:, :], src).then_inc(s_const, 16)

            pieced = Tally()
            negs = Tally()
            vs = Tally()
            accs = Tally()

            def stack(trip, ahead):
                u = ahead % STEPS
                pieced.add()
                sp.wait_ge(s_hi, pieced.at(trip, STEPS) * CHUNKS)
                sp.wait_ge(s_lo, pieced.at(trip, STEPS))
                for a, (tile, order) in enumerate(((qs[u], Q_PIECES), (ks[u], K_PIECES))):
                    for r, piece in enumerate(order):
                        sp.dma_start(tile[r * HD:(r + 1) * HD, :, :],
                                     pieces[a * 64:(a + 1) * 64, piece, :]).then_inc(s_stack, 16)
                group = 2 * dt_of(trip, ahead) + u % 2
                sp.dma_start(ks[u][ALIBI0:ALIBI0 + PIECES, :, :].rearrange("p h n -> p (h n)"),
                             alibi_d[bass.ds(group, 1)].rearrange("g p n -> (g p) n")).then_inc(s_stack, 16)

            def neg_rows(trip, ahead):
                u = ahead % STEPS
                negs.add()
                sp.wait_ge(s_negT, negs.at(trip, STEPS))
                sp.dma_start(qs[u][NEGMAX0:ROWS_ALL, :, :], negmaxT[:, :]).then_inc(s_negrows, 16)

            def store_raw(trip, u, c):
                accs.add()
                dt = dt_of(trip, u)
                g, b = u % 2, u // 2
                sp.wait_ge(s_acc_free, accs.at(trip, CHUNKS * STEPS) + 1)
                at = b * SEQ + c * CH
                sp.dma_start(att[g * 64:(g + 1) * 64, bass.ds(dt, 1), at:at + CH],
                             raw[c][0:P:2, :]).then_inc(s_raw[c], 16)
                sp.dma_start(sums_d[bass.ds(dt * DT_HEADS + g * HG, HG), at:at + CH],
                             raw[c][1:P:VC, :]).then_inc(s_raw[c], 16)

            sp.wait_ge(s_ones, 16 * 2)
            stack(0, 0)
            sp.wait_ge(s_xt, NT)
            sp.wait_ge(s_lp, 4 + 1 + 4)
            for t in (*qs[1:], *ks[1:]):
                sp.dma_start(t[ALIBI0:ROWS_ALL, :, :], ones_d).then_inc(s_ones, 16)
            sp.wait_ge(s_ones, 16 * 2 * STEPS)
            sp.wait_ge(s_le, 12)
            for g in range(GROUPS):
                sp.dma_start(bcat[g // 4][0:RANK, g % 4, :], beff[(g % 4) * RANK:(g % 4 + 1) * RANK, g // 4, :])\
                  .then_inc(s_bcat, 16)
            for t in bcat:
                sp.dma_start(t[RANK:RC, :, :], repeated(lbsT, 1, 4)).then_inc(s_bcat, 16)
            stack(0, 1)
            stack(0, 2)
            neg_rows(0, 0)
            vs.add(2)
            for c in range(CHUNKS):
                sp.sem_inc(s_raw[c], 32)

            def step(trip, u, last):
                plan = Plan(u, last)
                if not last and u < 2:
                    load_wqk(u, dt_of(trip, STEPS))
                if not last and u == 2:
                    sp.wait_ge(s_v, vs.at(trip, STEPS))
                    load_wv(dt_of(trip, STEPS))
                if plan.v:
                    vs.add()
                store_raw(trip, u, 0)
                if plan.neg:
                    neg_rows(trip, u + 1)
                if plan.qk:
                    stack(trip, u + 3)

            with sp.Fori(0, DTS - 1, 1) as trip:
                for u in range(STEPS):
                    step(trip, u, False)
                    store_raw(trip, u, 1)
            more = DTS - 2
            for t in (pieced, negs, vs):
                t.n += STEPS * more
            accs.n += CHUNKS * STEPS * more

            def sums_in(b):
                for c in range(CHUNKS):
                    sp.wait_ge(s_raw[c], 32 * (1 + STEPS * (DTS - 1) + 2 * (b + 1)))
                sp.dma_start(sums[b], sums_d[:, b * SEQ:(b + 1) * SEQ].rearrange("h (a n) -> h a n", n=256))\
                  .then_inc(s_sums, 16)

            def inverses(b):
                sp.wait_ge(s_inv, b + 1)
                sp.dma_start(inv_d[:, b * SEQ:(b + 1) * SEQ].rearrange("h (a n) -> h a n", n=256), inv[b])\
                  .then_inc(s_invst, 16)
                sp.wait_ge(s_invst, 16 * (b + 1))
                for dt in range(DTS):
                    src = inv_d[dt * DT_HEADS:(dt + 1) * DT_HEADS, b * SEQ:(b + 1) * SEQ]
                    sp.dma_start(invb[b][dt], bass.AP(tensor=src.tensor, offset=src.offset,
                                                      ap=[[TOK, DT_HEADS], [0, HD], [1, SEQ]])).then_inc(s_invb[b], 16)

            def load_xg(i):
                rows = slice(i * 4 * P, (i + 1) * 4 * P)
                sp.dma_start(xt[i][:, :, :], x[rows, :].rearrange("(t p) d -> p t d", p=P)).then_inc(s_xg[i], 16)
                sp.dma_start(gt[i][:, :, :], g_d[rows, :].rearrange("(t p) d -> p t d", p=P)).then_inc(s_xg[i], 16)

            for u in range(STEPS):
                if u == 2:
                    sums_in(0)
                step(DTS - 1, u, True)
                if u == 2:
                    inverses(0)
                store_raw(DTS - 1, u, 1)
                if u == 2:
                    sp.dma_start(wp, w_proj.rearrange("(k p) o -> p k o", p=P)).then_inc(s_wp, 16)
                    sp.wait_ge(s_z, NT)
                    sp.dma_start(bfb[:, :], row(b_proj)).then_inc(s_bp, 16)
                    for i in range(2):
                        sp.wait_ge(s_gst[i], 16 * 8)
                    sp.dma_start(xt[0][:, :, :], x[0:4 * P, :].rearrange("(t p) d -> p t d", p=P)).then_inc(s_xg[0], 16)
                    sp.dma_start(gt[0][:, :, :], g_d[0:4 * P, :].rearrange("(t p) d -> p t d", p=P)).then_inc(s_xg[0], 16)
            sums_in(1)
            inverses(1)
            for i in range(1, 4):
                load_xg(i)
            for i in range(NT):
                sp.wait_ge(s_res, i + 1)
                sp.dma_start(out[i * P:(i + 1) * P, :], xt[i // 4][:, i % 4, :]).then_inc(s_out, 16)
            sp.wait_ge(s_out, 16 * NT)

        @block.tensor
        def _(pe):
            def transposes(i):
                for t in range(4):
                    n = 4 * i + t
                    pe.wait_ge(s_xlo, n + 1)
                    if n >= 4:
                        pe.wait_ge(s_xte, n - 3)
                    for a in range(HALVES):
                        for k in range(KT):
                            o = (a * KT + k) * P
                            m = pe.transpose(ring[n % 4].bitcast(F16)[:, o:o + P], xp[i][:, a, t, k * P:(k + 1) * P],
                                             ident16[:, :])
                    m.then_inc(s_xt, 1)

            def largest_of(n, i):
                pe.wait_ge(s_col, 2 * i + 1)
                pe.transpose(mxp[i][0:n, 0:P], largest[:, 0:n], ident[:, :]).then_inc(s_row, 1)
                pe.wait_ge(s_col, 2 * i + 2)
                pe.matmul(mxp[i][:, P:P + n], onesf[0:n, :], diag[0:n, 0:n], start=True, stop=True).then_inc(s_row, 1)

            def lora_prep(between):
                uses = Tally()

                def bank():
                    if uses.n >= 4:
                        pe.wait_ge(s_le, uses.n - 3)
                    uses.add()
                    return ring[(uses.n - 1) % 4]

                pe.wait_ge(s_lora, 16 * 9)
                pe.wait_ge(s_gsel, 2)
                for it in range(KT):
                    b = bank()
                    for k in range(KT):
                        m = pe.matmul(b[:, 0:GROUPS * RANK], la[:, k, it * P:(it + 1) * P],
                                      gsel[:, k * 256:(k + 1) * 256], start=(k == 0), stop=(k == KT - 1))
                    m.then_inc(s_lp, 1)
                b = bank()
                for it in range(KT):
                    m = pe.transpose(b[:, it * RANK:(it + 1) * RANK], las[:, it * P:(it + 1) * P], ident[0:RANK, 0:RANK])
                m.then_inc(s_lp, 1)
                for k in range(KT):
                    b = bank()
                    for c in range(KT):
                        m = pe.transpose(b[:, c * P:(c + 1) * P], lbr[:, c, k * P:(k + 1) * P], ident[:, :])
                    m.then_inc(s_lp, 1)
                between()
                b = bank()
                for c in range(KT):
                    m = pe.transpose(b[0:RANK, c * P:(c + 1) * P], lbsr[:, c, :], ident[:, :])
                m.then_inc(s_lp, 1)
                for half in range(2):
                    b = bank()
                    if half == 0:
                        pe.wait_ge(s_le, 4 + 1 + 4)
                    for k in range(KT):
                        m = pe.matmul(b[:, :], gsel[:, k * 256 + half * P:k * 256 + (half + 1) * P], lbT[:, k, :],
                                      start=(k == 0), stop=(k == KT - 1))
                    m.then_inc(s_lp, 1)

            qks, vs, negTs = Tally(), Tally(), Tally()
            splits = Tally()
            stacked = Tally()
            maxed = Tally()
            negd = Tally()
            negrows = Tally()
            pairs = Tally()
            chunks = Tally()
            exps = Tally()
            held = []

            def misc_free(trip):
                if held:
                    s, tally, rate = held[-1]
                    pe.wait_ge(s, tally.at(trip, rate))

            def misc_used(ins, s, tally, rate):
                ins.then_inc(s_misc, 1)
                tally.add()
                held.append((s, tally, rate))

            def qk_part(trip, ahead, c, k):
                u = ahead % STEPS
                g, b = u % 2, u // 2
                if k == 0:
                    misc_free(trip)
                    if c == 0 and b == 0:
                        splits.add()
                        pe.wait_ge(s_wlo, splits.at(trip, 3))
                for wa, xa in PASSES:
                    m = pe.matmul(miscp[:, :], wqks[g][:, wa, k, :],
                                  xs[:, xa, k, b * SEQ + c * CH:b * SEQ + (c + 1) * CH],
                                  start=(k == 0 and (wa, xa) == PASSES[0]),
                                  stop=(k == KT - 1 and (wa, xa) == PASSES[-1]))
                if k == KT - 1:
                    misc_used(m, s_hi, qks, CHUNKS * STEPS)

            def v_part(trip, b, half, t):
                if t == 0:
                    misc_free(trip)
                    if half == 0 and b == 0:
                        splits.add()
                        pe.wait_ge(s_wlo, splits.at(trip, 3))
                tt = b * QT + half * 4 + t
                for k in range(KT):
                    for wa, xa in PASSES:
                        m = pe.matmul(miscp[:, t * P:(t + 1) * P], xs[:, xa, k, tt * P:(tt + 1) * P], wvs[:, wa, k, :],
                                      start=(k == 0 and (wa, xa) == PASSES[0]),
                                      stop=(k == KT - 1 and (wa, xa) == PASSES[-1]))
                if t == 3:
                    misc_used(m, s_v, vs, STEPS)

            def max_part(trip, ahead, i):
                u = ahead % STEPS
                h, t, c = MAXES[i]
                if i == 0:
                    stacked.add(16 * 13)
                    pe.wait_ge(s_stack, stacked.at(trip, 16 * 13 * STEPS))
                if maxed.n >= 2:
                    pe.wait_ge(s_mx_free, maxed.at(trip, NM * STEPS, 1))
                w = keys_of(t, c)
                pe.matmul(mxp[maxed.n % 2][:, 0:w], qs[u][0:ROWS_MAX, h, t * P:(t + 1) * P],
                          ks[u][0:ROWS_MAX, h, c * CH:c * CH + w], start=True, stop=True).then_inc(s_mx, 1)
                maxed.add()

            def neg_part(trip):
                misc_free(trip)
                negd.add()
                pe.wait_ge(s_neg, negd.at(trip, STEPS))
                m = pe.matmul(miscp[0:PIECES * HG * QT, 0:P], negmax[:, :, :].rearrange("p a b -> p (a b)"),
                              identb[:, :], start=True, stop=True)
                misc_used(m, s_negT, negTs, STEPS)

            def score_part(trip, u, n, pair):
                c, kb = UNITS[n]
                w = width(n)
                if n == 0 and pair == 0:
                    negrows.add(16)
                    pe.wait_ge(s_negrows, negrows.at(trip, 16 * STEPS))
                pe.wait_ge(s_exp, pairs.at(trip, 2 * NU * STEPS) + 1)
                for j in range(2):
                    h = 2 * pair + j
                    to = stp[pairs.n % 2][:, j, :]
                    m = pe.matmul(to[:, 0:w], ks[u][0:ROWS_ALL, h, kb * P:(kb + 1) * P],
                                  qs[u][0:ROWS_ALL, h, (c + 1) * CH - w:(c + 1) * CH], start=True,
                                  stop=not diagonal(n))
                    if diagonal(n):
                        m = pe.matmul(to[:, 0:P], identb[:, :], maskb[:, :], start=False, stop=True)
                m.then_inc(s_scores, 1)
                pairs.add()

            def pv_part(trip, u, n):
                c, kb = UNITS[n]
                w = width(n)
                g, b = u % 2, u // 2
                exps.add(2)
                pe.wait_ge(s_exp, exps.at(trip, 2 * NU * STEPS) + 2)
                if kb == 0:
                    chunks.add()
                    pe.wait_ge(s_acc_free, chunks.at(trip, CHUNKS * STEPS))
                for h in range(HG):
                    m = pe.matmul(accp[VC * h:VC * (h + 1), CH - w:CH], va[b][:, kb, g * HG + h, :],
                                  probs[(exps.n // 2 - 1) % 3][:, h, 0:w], start=(kb == 0),
                                  stop=(n == NU - 1 or UNITS[n + 1][0] != c))
                m.then_inc(s_pv, 1)

            pe.wait_ge(s_ident, 32)
            def qk_all(ahead, c):
                for k in range(KT):
                    qk_part(0, ahead, c, k)

            def v_all(half):
                for t in range(4):
                    v_part(0, 0, half, t)

            transposes(0)
            transposes(1)
            largest_of(1, 0)
            pe.wait_ge(s_xte, 8)
            qk_all(0, 0)
            transposes(2)
            qk_all(0, 1)
            v_all(0)
            transposes(3)
            v_all(1)
            largest_of(3, 1)
            qk_all(1, 0)
            pe.wait_ge(s_xte, NT)
            lora_prep(lambda: qk_all(1, 1))
            pe.wait_ge(s_le, 12)
            for i in range(4):
                for j in range(2):
                    g = 2 * i + j
                    for k in range(KT):
                        for aa, xa in PASSES:
                            m = pe.matmul(ring[i][0:RC, j * GTOK:(j + 1) * GTOK], acat[:, aa, k, g, :],
                                          xs[:, xa, k, g * GTOK:(g + 1) * GTOK],
                                          start=(k == 0 and (aa, xa) == PASSES[0]),
                                          stop=(k == KT - 1 and (aa, xa) == PASSES[-1]))
                m.then_inc(s_ax, 1)
            pe.wait_ge(s_const, 16 * 4)
            splits.add()
            pe.wait_ge(s_wlo, splits.n)
            pe.wait_ge(s_bcat, 16 * (GROUPS + 2))
            todo = list(FIRST_MAXES)
            for i in range(NT):
                g = i * P // GTOK
                if i == 0:
                    pe.wait_ge(s_axe, 4)
                if i >= 4:
                    pe.wait_ge(s_z, i - 3)
                for k in range(KT + 1):
                    if k < KT:
                        for wa, xa in PASSES:
                            m = pe.matmul(ring[i % 4], xs[:, xa, k, i * P:(i + 1) * P], wfs[:, wa, k, :],
                                          start=(k == 0 and (wa, xa) == PASSES[0]), stop=False)
                    else:
                        m = pe.matmul(ring[i % 4], axT[0:RC, i * P:(i + 1) * P], bcat[g // 4][:, g % 4, :],
                                      start=False, stop=True)
                    if todo:
                        max_part(0, *todo.pop(0))
                m.then_inc(s_ff, 1)
                if i in QK_AT:
                    qk_all(2, QK_AT.index(i))
                if i == NEG_AT + 1:
                    neg_part(0)
            assert not todo
            pe.sem_inc(s_pv, 3)
            pe.wait_ge(s_z, NT)
            for pair in range(2):
                score_part(0, 0, 0, pair)

            def fill(trip, u, n, plan):
                for what, *at in FILL.get(n, ()):
                    if what == "qk" and plan.qk:
                        qk_part(trip, u + 3, *at)
                    if what == "neg" and plan.neg:
                        neg_part(trip)
                    if what == "v" and plan.v:
                        v_part(trip, (u // 2 + 1) % 2, u % 2, *at)

            held.append((s_v, vs, STEPS))

            def step(trip, u, last):
                plan = Plan(u, last)
                for n in range(NU):
                    todo = maxes_of(n, plan.near, plan.far)
                    for pair in range(2):
                        if n < NU - 1:
                            score_part(trip, u, n + 1, pair)
                        elif plan.neg:
                            score_part(trip, (u + 1) % STEPS, 0, pair)
                        if todo:
                            max_part(trip, u + todo[0][0], todo.pop(0)[1])
                    if n not in LATE:
                        fill(trip, u, n, plan)
                    if n in FILL and n not in LATE and todo:
                        max_part(trip, u + todo[0][0], todo.pop(0)[1])
                    pv_part(trip, u, n)
                    if todo:
                        max_part(trip, u + todo[0][0], todo.pop(0)[1])
                    if n in LATE:
                        fill(trip, u, n, plan)
                    while todo:
                        max_part(trip, u + todo[0][0], todo.pop(0)[1])

            with pe.Fori(0, DTS - 1, 1) as trip:
                for u in range(STEPS):
                    step(trip, u, False)
            more = DTS - 2
            qks.n += CHUNKS * STEPS * more
            for t in (vs, negTs, negd):
                t.n += STEPS * more
            splits.n += 3 * more
            stacked.n += 16 * 13 * STEPS * more
            maxed.n += NM * STEPS * more
            pairs.n += 2 * NU * STEPS * more
            exps.n += 2 * NU * STEPS * more
            chunks.n += CHUNKS * STEPS * more
            negrows.n += 16 * STEPS * more
            for u in range(STEPS):
                step(DTS - 1, u, True)

            pe.wait_ge(s_exp, 2 + pairs.n)
            pe.wait_ge(s_wp, 16)
            for i in range(NT):
                if i % (NT // BATCH) == 0:
                    pe.wait_ge(s_att, DTS * (i // (NT // BATCH) + 1))
                if i >= 4:
                    pe.wait_ge(s_y, i - 3)
                for k in range(KT):
                    m = pe.matmul(ring[i % 4], att[:, k, i * P:(i + 1) * P], wp[:, k, :], start=(k == 0), stop=(k == KT - 1))
                m.then_inc(s_op, 1)

        @block.scalar
        def _(act):
            def roots(i):
                act.wait_ge(s_var, i + 1)
                act.activation(std[:, :], meanvar[:, :, 1], ACT.Sqrt, scale=1 / X_SCALE ** 2).then_inc(s_std, 1)

            def first_pieces(i):
                for t in range(4):
                    act.wait_ge(s_xn, 4 * i + t + 1)
                    act.activation(xp[i][:, 0, t, :], xin[i][:, t, :], ACT.Copy).then_inc(s_xhi, 1)

            scalings = Tally()

            def weights_out(trip, pieces_t, whole, weight_scale, s, count):
                flat = whole[:, :, :].rearrange("p k n -> p (k n)")
                act.wait_ge(s, count)
                act.activation(flat, flat, ACT.Identity, scale=weight_scale).then_inc(s_wscaled, 1)
                scalings.add()
                act.wait_ge(s_wscaled, scalings.at(trip, 3))
                act.activation(pieces_t[:, 0].rearrange("p k n -> p (k n)"), flat, ACT.Copy).then_inc(s_whi, 1)

            def transposed(i):
                for t in range(4):
                    n = 4 * i + t
                    act.wait_ge(s_xt, n + 1)
                    act.activation(xs[:, :, :, n * P:(n + 1) * P].rearrange("p a k n -> p (a k) n"),
                                   ring[n % 4].bitcast(F16).rearrange("p (b m) -> p b m", m=P), ACT.Copy)\
                       .then_inc(s_xte, 1)

            miscs = Tally()
            stacked = Tally()
            pairs = Tally()
            used = Tally()
            negs = Tally()
            RM = (CHUNKS + 2) * STEPS

            def misc_full(trip):
                miscs.add()
                act.wait_ge(s_misc, miscs.at(trip, RM))

            def qk_out(trip, ahead, c):
                g = ahead % 2
                if c == 0 and stacked.n:
                    act.wait_ge(s_stack, stacked.at(trip, 16 * 13 * STEPS))
                misc_full(trip)
                part = slice(c * CH, (c + 1) * CH)
                act.activation(qk[:, part], miscp[:, :], ACT.Identity, bias=bqk[g][:, 0:1], scale=back[:, 0:1])
                act.activation(pieces[:, 0, part], miscp[:, :], ACT.Identity, bias=bqk[g][:, 0:1],
                               scale=back[:, 0:1]).then_inc(s_hi, 1)
                if c == 1:
                    stacked.add(16 * 13)

            def v_out(trip, b, half):
                misc_full(trip)
                act.activation(va[b][:, half * 4:(half + 1) * 4, :, :].rearrange("p t h (d e) -> p (t h d) e", e=2)[:, :, 0],
                               miscp[:, :], ACT.Identity, scale=back[:, 0:1]).then_inc(s_v, 1)

            def neg_out(trip):
                misc_full(trip)
                if negs.n:
                    act.wait_ge(s_negrows, negs.at(trip, 16 * STEPS))
                act.activation(negmaxT[:, :], miscp[0:PIECES * HG * QT, 0:P], ACT.Copy).then_inc(s_negT, 1)
                negs.add(16)

            wloads = [Tally(), Tally()]
            vloads = Tally()

            def wqk_out(trip, g):
                wloads[g].add(32)
                weights_out(trip, wqks[g], wqk[g], scale[:, 0:1], s_w[g], wloads[g].at(trip, 32))

            def wv_out(trip):
                vloads.add(16)
                weights_out(trip, wvs, wv, scale[:, 0:1], s_wv, vloads.at(trip, 16))

            roots(0)
            first_pieces(0)
            roots(1)
            transposed(0)
            first_pieces(1)
            transposed(1)
            act.wait_ge(s_scale, 1)
            wqk_out(0, 0)
            wv_out(0)
            roots(2)
            wqk_out(0, 1)
            first_pieces(2)
            qk_out(0, 0, 0)
            roots(3)
            transposed(2)
            qk_out(0, 0, 1)
            first_pieces(3)
            v_out(0, 0, 0)
            transposed(3)
            v_out(0, 0, 1)
            act.wait_ge(s_scale, 2)
            weights_out(0, wfs, wf, scale[:, 1:2], s_wf, 32)
            for c in range(CHUNKS):
                qk_out(0, 1, c)
            for i in range(4):
                act.wait_ge(s_ax, i + 1)
                act.activation(axT[0:RC, i * CH:(i + 1) * CH], ring[i][0:RC, :], ACT.Identity,
                               scale=ratio[0:RC, :]).then_inc(s_axe, 1)
            for i in range(NT):
                act.wait_ge(s_z, i + 1)
                if i == 8:
                    act.wait_ge(s_gst[0], 16 * 8)
                act.activation(g_t[i % 8], z_t[i % 2][:, :], ACT.Silu).then_inc(s_g, 1)
                act.wait_ge(s_g, i + 1)
                act.dma_start(g_d[i * P:(i + 1) * P, :], g_t[i % 8]).then_inc(s_gst[i // 8], 16)
                if i in QK_AT:
                    qk_out(0, 2, QK_AT.index(i))
                if i == NEG_AT + 1:
                    neg_out(0)
            act.sem_inc(s_exp, 2)

            def step(trip, u, last):
                plan = Plan(u, last)
                for n in range(NU):
                    w = width(n)
                    buf = probs[used.n % 3]
                    act.wait_ge(s_pv, used.at(trip, NU * STEPS) + 1)
                    for pair in range(2):
                        i = pairs.n
                        pairs.add()
                        act.wait_ge(s_scores, pairs.at(trip, 2 * NU * STEPS))
                        act.activation(buf[:, 2 * pair:2 * pair + 2, 0:w], stp[i % 2][:, :, 0:w], ACT.Exp,
                                       scale=SCALE).then_inc(s_exp, 1)
                    used.add()
                    if u == 0 and n == 0:
                        act.wait_ge(s_gst[1], 16 * 8)
                    if n == WEIGHTS_AT and not last and u < 2:
                        wqk_out(trip, u)
                    if n == WEIGHTS_AT and not last and u == 2:
                        wv_out(trip)
                    what, *at = EMPTY.get(n, ("",))
                    if what == "qk" and plan.qk:
                        qk_out(trip, u + 3, *at)
                    if what == "neg" and plan.neg:
                        neg_out(trip)
                    if what == "v" and plan.v:
                        v_out(trip, (u // 2 + 1) % 2, u % 2)

            with act.Fori(0, DTS - 1, 1) as trip:
                for u in range(STEPS):
                    step(trip, u, False)
            more = DTS - 2
            for t in wloads:
                t.n += 32 * more
            vloads.n += 16 * more
            scalings.n += 3 * more
            miscs.n += RM * more
            stacked.n += 16 * 13 * STEPS * more
            pairs.n += 2 * NU * STEPS * more
            used.n += NU * STEPS * more
            negs.n += 16 * STEPS * more
            for u in range(STEPS):
                step(DTS - 1, u, True)

        @block.vector
        def _(dve):
            larges = Tally()

            def link_large():
                larges.add()
                dve.wait_ge(s_large, larges.n)

            def largest_to(col, t, parts=P):
                dve.tensor_reduce(largest[0:parts, col:col + 1], t, AX.X, ALU.max, apply_absolute_value=True)\
                   .then_inc(s_large, 1)
                link_large()

            def over_all(n, i):
                dve.sem_inc(s_col, 1)
                dve.wait_ge(s_row, 2 * i + 1)
                dve.tensor_reduce(largest[0:n, 7:8], mxp[i][0:n, 0:P], AX.X, ALU.max).then_inc(s_large, 1)
                link_large()
                dve.tensor_scalar(diag[0:n, 0:n], ident[0:n, 0:n], largest[0:n, 7:8], None, ALU.mult).then_inc(s_col, 1)
                dve.wait_ge(s_row, 2 * i + 2)

            def scales(lo, hi):
                e, r = power[:, lo:hi], inverse_p[:, lo:hi]
                dve.tensor_scalar(bound[:, lo:hi], bound[:, lo:hi], SMALLEST, None, ALU.max).then_inc(s_large, 1)
                link_large()
                dve.tensor_scalar(e.bitcast(I32), bound[:, lo:hi].bitcast(I32), EXPONENT, None, ALU.bitwise_and)\
                   .then_inc(s_large, 1)
                link_large()
                dve.reciprocal(r, e).then_inc(s_large, 1)
                link_large()
                dve.tensor_scalar(r, r, 1 + 2.0 ** -10, None, ALU.mult).then_inc(s_large, 1)
                link_large()
                dve.tensor_scalar(r.bitcast(I32), r.bitcast(I32), EXPONENT, None, ALU.bitwise_and).then_inc(s_large, 1)
                link_large()
                dve.tensor_scalar(back[:, lo:hi], e, 1 / (W_SCALE * X_SCALE), None, ALU.mult)
                dve.tensor_scalar(scale[:, lo:hi], r, W_SCALE, None, ALU.mult).then_inc(s_scale, 1)

            for i in range(4):
                dve.wait_ge(s_x[i], 16)
                for t in range(4):
                    if i == 0 and t == 2:
                        dve.wait_ge(s_x[4], 16)
                    dve.bn_stats(stats[:, t, :], xin[i][:, t, :]).then_inc(s_stats, 1)
                dve.wait_ge(s_stats, 5 * i + 4)
                for t in range(4):
                    m = dve.bn_aggr(meanvar[:, t, :], stats[:, t, :])
                m.then_inc(s_stats, 1)
                dve.wait_ge(s_stats, 5 * i + 5)
                dve.tensor_scalar(meanvar[:, :, 1], meanvar[:, :, 1], EPS, None, ALU.add).then_inc(s_var, 1)
                dve.wait_ge(s_std, i + 1)
                dve.reciprocal(rstd[:, :], std[:, :]).then_inc(s_rstd, 1)
                dve.wait_ge(s_rstd, i + 1)
                for t in range(4):
                    dve.tensor_scalar(xin[i][:, t, :], xin[i][:, t, :], meanvar[:, t, 0:1], rstd[:, t:t + 1],
                                      ALU.subtract, ALU.mult).then_inc(s_xn, 1)
                if i == 0:
                    dve.memset(onesf[:, :], 1.0)
                if i == 1:
                    dve.memset(va[0][:, :, :, :].rearrange("p t h (d e) -> p (t h d) e", e=2)[:, :, 1], 1.0)
                    dve.memset(tops[:, :, :], NEG)
                    dve.wait_ge(s_watt, 32)
                    largest_to(0, watt)
                    over_all(1, 0)
                    dve.tensor_copy(bound[:, 0:1], mxp[0][:, P:P + 1]).then_inc(s_large, 1)
                    link_large()
                    scales(0, 1)

            dve.wait_ge(s_lora, 16 * 9)
            dve.wait_ge(s_lora, 16 * 9)
            dve.wait_ge(s_wf, 32)
            dve.memset(largest[:, 2:3], 0.0)
            largest_to(0, wf[:, :, :].rearrange("p k o -> p (k o)"))
            largest_to(1, la.rearrange("p k i -> p (k i)"))
            largest_to(2, las[:, :], RANK)
            largest_to(3, gateall)
            over_all(3, 1)
            dve.tensor_copy(bound[:, 1:2], mxp[1][:, P:P + 1])
            dve.tensor_scalar(bound[:, 2:3], mxp[1][:, P + 1:P + 2], largest[:, 3:4], float(LORAS), ALU.mult, ALU.mult)\
               .then_inc(s_large, 1)
            link_large()
            dve.tensor_tensor(bound[:, 2:3], bound[:, 2:3], mxp[1][:, P + 2:P + 3], ALU.max).then_inc(s_large, 1)
            link_large()
            scales(1, 3)
            dve.wait_ge(s_scale, 2)
            dve.tensor_scalar(ratio[:, :], power[:, 2:3], inverse_p[:, 1:2], None, ALU.mult).then_inc(s_large, 1)
            for n in range(LORAS):
                k, p0 = n // 4, (n % 4) * RANK
                m = dve.tensor_copy(gatep[p0:p0 + RANK, k * GROUPS:(k + 1) * GROUPS],
                                     gateall[p0:p0 + RANK, n:GROUPS * LORAS:LORAS])
            m.then_inc(s_gsel, 1)
            dve.wait_ge(s_gsel, 1)
            dve.wait_ge(s_xlo, NT)
            dve.tensor_tensor(gsel.rearrange("p (g r) -> p g r", r=RANK), repeated(pick, 1, KT * GROUPS),
                              repeated(gatep, 2, RANK), ALU.mult).then_inc(s_gsel, 1)

            uses = Tally()

            def bank():
                uses.add()
                dve.wait_ge(s_lp, uses.n)
                return ring[(uses.n - 1) % 4]

            def pieces_of(to_hi, to_lo, what, hi_again):
                dve.tensor_scalar(to_hi, what, scale[:, 2:3], None, ALU.mult).then_inc(s_large, 1)
                link_large()
                return dve.scalar_tensor_tensor(out=to_lo, in0=what, scalar=scale[:, 2:3], in1=hi_again,
                                                op0=ALU.mult, op1=ALU.subtract)

            larges.add()
            for it in range(KT):
                own = acat[:, :, it, :, 0:RANK]
                pieces_of(own[:, 0], own[:, 1], bank()[:, 0:256].rearrange("p (g r) -> p g r", g=GROUPS), own[:, 0])\
                    .then_inc(s_le, 1)
            b = bank()
            for k in range(KT):
                shared = acat[:, :, k, :, RANK:RC]
                m = pieces_of(shared[:, 0], shared[:, 1], repeated(b[:, k * RANK:(k + 1) * RANK], 1, GROUPS), shared[:, 0])
            m.then_inc(s_le, 1)
            for k in range(KT):
                dve.tensor_copy(lbT[:, k, :], bank()[:, :]).then_inc(s_le, 1)
            dve.tensor_copy(lbsT[:, :], bank()[0:RANK, :]).then_inc(s_le, 1)
            for half in range(2):
                dve.tensor_copy(beff[:, half, :], bank()[:, :]).then_inc(s_le, 1)

            maxed = Tally()
            links = Tally()
            negs = Tally()
            pvs = Tally()
            rawd = Tally()

            def max_part(trip, i):
                h, t, c = MAXES[i]
                w = keys_of(t, c)
                bank = mxp[maxed.n % 2]
                maxed.add()
                dve.wait_ge(s_mx, maxed.at(trip, NM * STEPS))
                to = tops[:, c, h * QT + t:h * QT + t + 1]
                if t // CT == c:
                    dve.sem_inc(s_seen, 1)
                    m = dve.tensor_tensor_reduce(junk[:, (maxed.n - 1) % 2, 0:w], bank[:, 0:w], mask[:, CH - w:CH],
                                                 1.0, NEG, ALU.add, ALU.max, to)
                else:
                    m = dve.tensor_reduce(to, bank[:, 0:w], AX.X, ALU.max)
                m.then_inc(s_mx_free, 1)

            def neg_part(trip, link):
                if link == 0:
                    dve.wait_ge(s_mx_free, maxed.at(trip, NM * STEPS))
                    if negs.n:
                        dve.wait_ge(s_negT, negs.at(trip, STEPS))
                    negs.add()
                    ins = dve.tensor_tensor(top[:, :], tops[:, 0, :], tops[:, 1, :], ALU.max)
                else:
                    dve.wait_ge(s_top, links.at(trip, (LINKS - 1) * STEPS))
                if link == 1:
                    ins = dve.tensor_scalar(negmax[:, 0, :], top[:, :], -1.0, None, ALU.mult)
                if link == 2:
                    ins = dve.scalar_tensor_tensor(out=toprest[:, :], in0=top[:, :], scalar=-1.0,
                                                   in1=negmax[:, 0, :], op0=ALU.mult, op1=ALU.subtract)
                if link == 3:
                    ins = dve.tensor_copy(negmax[:, 1, :], toprest[:, :])
                if link < LINKS - 1:
                    ins.then_inc(s_top, 1)
                    links.add()
                else:
                    dve.tensor_tensor(negmax[:, 2, :], toprest[:, :], negmax[:, 1, :], ALU.subtract).then_inc(s_neg, 1)

            def acc_out(trip, c):
                pvs.add(CT * (c + 1))
                dve.wait_ge(s_pv, pvs.at(trip, NU * STEPS) + 3)
                if c == 0:
                    rawd.add(32)
                dve.wait_ge(s_raw[c], rawd.at(trip, 32 * STEPS))
                dve.tensor_copy(raw[c][:, :], accp[:, :]).then_inc(s_acc_free, 1)

            dve.wait_ge(s_const, 16 * 4)
            dve.wait_ge(s_wf, 32)
            todo = list(FIRST_MAXES)

            def z_out(i):
                dve.wait_ge(s_ff, i + 1)
                if i >= 2:
                    dve.wait_ge(s_g, i - 1)
                dve.scalar_tensor_tensor(out=z_t[i % 2][:, :], in0=ring[i % 4], scalar=back[:, 1:2], in1=bfb[:, :],
                                         op0=ALU.mult, op1=ALU.add).then_inc(s_z, 1)

            for i in range(NT):
                for j in range(PER_FFN):
                    if todo:
                        max_part(0, todo.pop(0)[1])
                    if len(todo) == len(FIRST_MAXES) - NM and not negs.n:
                        for link in range(LINKS):
                            neg_part(0, link)
                    if j == 1 and i:
                        z_out(i - 1)
                if i == 0:
                    dve.wait_ge(s_bcat, 16 * (GROUPS + 2))
                    dve.memset(va[1][:, :, :, :].rearrange("p t h (d e) -> p (t h d) e", e=2)[:, :, 1], 1.0)
            z_out(NT - 1)
            dve.wait_ge(s_g, NT)
            dve.sem_inc(s_acc_free, 1)

            def step(trip, u, last):
                plan = Plan(u, last)
                for n in range(NU):
                    if n == CT:
                        acc_out(trip, 0)
                    todo = maxes_of(n, plan.near, plan.far)
                    for j in range(PER_UNIT):
                        if plan.neg and n == HALF_U:
                            for link in (0, 1) if j == 0 else (j + 1,):
                                neg_part(trip, link)
                        if todo:
                            max_part(trip, todo[j][1])
                    if last and u == 2 and n == HALF_U:
                        inverse(0)
                    if last and u == 3 and n == CT:
                        normalise(0)
                acc_out(trip, 1)

            def inverse(b):
                dve.wait_ge(s_sums, 16 * (b + 1))
                dve.reciprocal(inv[b], sums[b]).then_inc(s_inv, 1)

            def normalise(b):
                dve.wait_ge(s_invb[b], 16 * DTS)
                part = slice(b * SEQ, (b + 1) * SEQ)
                for dt in range(DTS):
                    dve.tensor_tensor(att[:, dt, part], att[:, dt, part], invb[b][dt], ALU.mult).then_inc(s_am, 1)
                    dve.wait_ge(s_am, DTS * b + dt + 1)
                    dve.tensor_scalar(att[:, dt, part], att[:, dt, part], bv[:, dt:dt + 1], None, ALU.add)\
                       .then_inc(s_att, 1)

            with dve.Fori(0, DTS - 1, 1) as trip:
                for u in range(STEPS):
                    step(trip, u, False)
            more = DTS - 2
            maxed.n += NM * STEPS * more
            links.n += (LINKS - 1) * STEPS * more
            negs.n += STEPS * more
            pvs.n += NU * STEPS * more
            rawd.n += 32 * STEPS * more
            for u in range(STEPS):
                step(DTS - 1, u, True)

            inverse(1)
            dve.wait_ge(s_bp, 16)
            for i in range(NT):
                if i == 4:
                    normalise(1)
                dve.wait_ge(s_op, i + 1)
                y, last = y_t[i % 4], xt[i // 4][:, i % 4, :]
                dve.tensor_tensor(y, ring[i % 4], bfb[:, :], ALU.add).then_inc(s_y, 1)
                dve.wait_ge(s_y, i + 1)
                dve.wait_ge(s_xg[i // 4], 32)
                dve.tensor_tensor(y, y, gt[i // 4][:, i % 4, :], ALU.mult).then_inc(s_yg, 1)
                dve.wait_ge(s_yg, i + 1)
                dve.tensor_tensor(last, y, last, ALU.add).then_inc(s_res, 1)

        @block.gpsimd
        def _(pool):
            hi = Tally()
            mids = Tally()

            def split(trip):
                hi.add(CHUNKS)
                pool.wait_ge(s_hi, hi.at(trip, CHUNKS * STEPS))
                pool.tensor_tensor(pieces[:, 1, :], qk[:, :], pieces[:, 0, :], ALU.subtract).then_inc(s_mid, 1)
                mids.add()
                pool.wait_ge(s_mid, mids.at(trip, STEPS))
                pool.tensor_tensor(qk[:, :], qk[:, :], pieces[:, 0, :], ALU.subtract).then_inc(s_rest, 1)
                pool.wait_ge(s_rest, mids.at(trip, STEPS))
                pool.tensor_tensor(pieces[:, 2, :], qk[:, :], pieces[:, 1, :], ALU.subtract).then_inc(s_lo, 1)

            his = Tally()

            def last_pieces(i):
                for t in range(4):
                    pool.wait_ge(s_xhi, 4 * i + t + 1)
                    pool.tensor_tensor(xp[i][:, 1, t, :], xin[i][:, t, :], xp[i][:, 0, t, :], ALU.subtract)\
                        .then_inc(s_xlo, 1)

            def weights_split(trip, pieces_t, whole):
                his.add()
                pool.wait_ge(s_whi, his.at(trip, 3))
                flat = [t.rearrange("p k n -> p (k n)") for t in (whole[:, :, :], pieces_t[:, 0], pieces_t[:, 1])]
                pool.tensor_tensor(flat[2], flat[0], flat[1], ALU.subtract).then_inc(s_wlo, 1)

            last_pieces(0)
            last_pieces(1)
            weights_split(0, wqks[0], wqk[0])
            weights_split(0, wvs, wv)
            weights_split(0, wqks[1], wqk[1])
            last_pieces(2)
            last_pieces(3)
            split(0)
            weights_split(0, wfs, wf)
            split(0)
            split(0)

            def step(trip, u, last):
                if not last and u < 2:
                    weights_split(trip, wqks[u], wqk[u])
                if not last and u == 2:
                    weights_split(trip, wvs, wv)
                if Plan(u, last).qk:
                    split(trip)

            with pool.Fori(0, DTS - 1, 1) as trip:
                for u in range(STEPS):
                    step(trip, u, False)
            hi.n += CHUNKS * STEPS * (DTS - 2)
            his.n += 3 * (DTS - 2)
            mids.n += STEPS * (DTS - 2)
            for u in range(STEPS):
                step(DTS - 1, u, True)


_INS = ["L0_attn_hidden_states", "L0_attn_w_attn", "L0_attn_b_attn", "L0_attn_w_proj", "L0_attn_b_proj",
        "L0_ffn_gate", "L0_ffn_kernel", "L0_ffn_bias", "L0_ffn_lora_A", "L0_ffn_lora_B",
        "L0_ffn_lora_A_shared", "L0_ffn_lora_B_shared"]


def _constants():
    import numpy as np

    bf = np.dtype("bfloat16")
    ident = np.eye(P, dtype=np.float32)
    mask = np.zeros((P, CH), np.float32)
    mask[:, CH - P:] = np.where(np.arange(P)[None, :] > np.arange(P)[:, None], np.float32(NEG), np.float32(0))
    maskb = np.where(np.arange(P)[:, None] > np.arange(P)[None, :], np.float32(-1e30), np.float32(0)).astype(bf)
    slopes = (np.float32(2 ** (-2 ** (-(5 - 3)))) ** np.arange(1, HEADS + 1, dtype=np.float32)).astype(np.float32)
    term = (slopes[:, None] * np.arange(SEQ, dtype=np.float32)[None, :] / np.float32(SCALE)).astype(np.float32)
    parts = []
    for _ in range(PIECES):
        part = term.astype(bf)
        parts.append(part)
        term = term - part.astype(np.float32)
    alibi = np.stack(parts, 1).reshape(HEADS // HG, HG, PIECES, SEQ).transpose(0, 2, 1, 3)
    pick = np.tile(np.eye(RANK, dtype=np.float32), (P // RANK, 1))
    return {"c_ident": ident, "c_ident16": ident.astype(np.float16), "c_identb": ident.astype(bf), "c_mask": mask, "c_maskb": maskb,
            "c_alibi": np.ascontiguousarray(alibi.reshape(HEADS // HG, PIECES, HG * SEQ)), "c_pick": pick, "c_ones": np.ones((2 * PIECES, HG, SEQ), bf)}


def _by_group(w, b):
    import numpy as np

    w = w.reshape(HID, 3, HEADS // HG, HG, HD)
    b = b.reshape(3, HEADS // HG, HG, HD)
    return {"w_qk": np.ascontiguousarray(w[:, :2].transpose(2, 0, 1, 4, 3).reshape(HEADS // HG, HID, P)),
            "b_qk": np.ascontiguousarray(b[:2].transpose(1, 0, 3, 2).reshape(HEADS // HG, P)),
            "w_v": np.ascontiguousarray(w[:, 2].reshape(HID, HID)),
            "b_v": np.ascontiguousarray(b[2].reshape(KT, P).T)}


def kernel(**inputs):
    import numpy as np
    import concourse.bacc as bacc
    from concourse.bass_utils import run_bass_kernel_spmd

    nc = bacc.Bacc("TRN2", target_bir_lowering=False, num_devices=1)
    arrays = {f"in_{name}": np.ascontiguousarray(inputs[name]) for name in _INS if "_attn_w_attn" not in name
              and "_attn_b_attn" not in name}
    arrays.update(_by_group(np.asarray(inputs["L0_attn_w_attn"]), np.asarray(inputs["L0_attn_b_attn"])))
    arrays.update(_constants())
    args = {name: nc.dram_tensor(name, a.shape, mybir.dt.from_np(a.dtype), kind="ExternalInput").ap()
            for name, a in arrays.items()}
    out = nc.dram_tensor("out", [TOK, HID], F32, kind="ExternalOutput").ap()
    flat = args["in_L0_attn_hidden_states"].rearrange("b s d -> (b s) d")
    rest = [args[f"in_{name}"] for name in _INS[3:]]
    attention_and_gate(nc, flat, args["w_qk"], args["w_v"], args["b_qk"], args["b_v"], *rest, args["c_ident"], args["c_ident16"], args["c_identb"], args["c_mask"], args["c_maskb"], args["c_alibi"],
                       args["c_pick"], args["c_ones"], out)
    got = run_bass_kernel_spmd(nc, [arrays], core_ids=[0])
    return got.results[0]["out"].reshape(BATCH, SEQ, HID)
```

```python
from contextlib import ExitStack

import concourse.bass as bass
from concourse import mybir

F32 = mybir.dt.float32
BF16 = mybir.dt.bfloat16
F16 = mybir.dt.float16
I32 = mybir.dt.int32
ALU = mybir.AluOpType
AX = mybir.AxisListType
ACT = mybir.ActivationFunctionType

P = 128
BATCH, SEQ, HID = 2, 1024, 512
TOK = BATCH * SEQ
HEADS = 32
HD = HID // HEADS
KT = HID // P
HG = 4
DT_HEADS = P // HD
DTS = HEADS // DT_HEADS
STEPS = 4
CH = 512
CHUNKS = SEQ // CH
QT = SEQ // P
CT = CH // P
PIECES = 3
PROD = 6 * HD
ALIBI0 = PROD
NEGMAX0 = PROD + PIECES
ROWS_MAX = NEGMAX0
ROWS_ALL = NEGMAX0 + PIECES
Q_PIECES = [0, 0, 0, 1, 1, 2]
K_PIECES = [0, 1, 2, 0, 1, 0]
SCALE = 1.0 / HD
NEG = -3.0e38
EPS = 1e-5
HALVES = 2
PASSES = [(0, 0), (0, 1), (1, 0)]
X_SCALE = 2.0 ** 11
W_SCALE = 2.0 ** 14
EXPONENT = 0x7F800000
SMALLEST = 1e-18
VC = 2 * HD

LORAS, RANK, GROUPS = 16, 32, 8
GTOK = TOK // GROUPS
RC = 2 * RANK

UNITS = [(c, kb) for c in range(CHUNKS) for kb in range(CT * (c + 1))]
NU = len(UNITS)
ITEMS = sorted(((t, c) for t in range(QT) for c in range(t // CT + 1)),
               key=lambda item: min(CH, (item[0] + 1) * P - item[1] * CH))
PER_UNIT = HG * len(ITEMS) // NU
SHARE = len(ITEMS) // PER_UNIT
MAXES = [(h, *item) for h in range(HG) for i in range(SHARE)
         for item in (ITEMS[2 * SHARE - 1 - i], ITEMS[2 * SHARE + 2 * i], ITEMS[2 * SHARE + 2 * i + 1], ITEMS[i])]
NM = len(MAXES)
HALF_U, HALF_M = NU // 2, NM // 2
PER_FFN = 5
FIRST_MAXES = [(0, i) for i in range(NM)] + [(1, i) for i in range(HALF_M)]
PARTS = [(1, range(DTS - 1)), (0, range(DTS)), (1, range(DTS - 1, DTS))]
NORMAL_AT = {0: (0, 0), 2: (0, 1), **{CT + n: at for n, at in enumerate([(0, 2), *((1, j) for j in range(DTS))])}}
LINKS = 5
NT = TOK // P
QK_AT = (3, 7)
NEG_AT = -(-NM // PER_FFN)


FILL = {0: [("qk", 0, 0)], 1: [("qk", 0, 1)], 2: [("qk", 0, 2), ("qk", 0, 3)],
        3: [("qk", 1, 0)], 4: [("qk", 1, 1)], 5: [("qk", 1, 2)], 6: [("qk", 1, 3)],
        7: [("neg",)], 8: [("v", 0)], 9: [("v", 1)], 10: [("v", 2), ("v", 3)]}
LATE = (3, 7, 8)
WEIGHTS_AT = 2
EMPTY = {3: ("qk", 0), 7: ("qk", 1), 8: ("neg",), 11: ("v",)}


def width(n):
    c, kb = UNITS[n]
    return CH - max(0, kb - CT * c) * P


def diagonal(n):
    c, kb = UNITS[n]
    return kb >= CT * c


def maxes_of(n, near, far):
    if n < HALF_U:
        return [(1, HALF_M + PER_UNIT * n + i) for i in range(PER_UNIT)] if near else []
    return [(2, PER_UNIT * (n - HALF_U) + i) for i in range(PER_UNIT)] if far else []


def keys_of(t, c):
    return min(CH, (t + 1) * P - c * CH)


class Plan:

    def __init__(self, u, last):
        after = STEPS - 1 - u if last else STEPS
        self.near, self.far = after >= 1, after >= 2
        self.qk = after >= 3
        self.v = after >= 2
        self.neg = after >= 1


class Tally:

    def __init__(self, n=0):
        self.n = n

    def add(self, k=1):
        self.n += k
        return self.n

    def at(self, trip, rate, less=0):
        v = self.n - less
        return v if isinstance(trip, int) else trip * rate + v


def attention_and_gate(nc, x, w_qk, w_v, b_qk, b_v, w_proj, b_proj, gate, w_ffn, b_ffn, lora_a, lora_b,
                       lora_as, lora_bs, ident_d, ident16_d, identb_d, mask_d, maskb_d, alibi_d, pick_d, ones_d, out):
    ctx = ExitStack()
    with ctx:
        def sb(name, shape, dt):
            return ctx.enter_context(nc.sbuf_tensor(name, shape, dt))

        def sem(name):
            return ctx.enter_context(nc.semaphore(name))

        sums_d = nc.dram_tensor("sums_d", [HEADS, TOK], F32, kind="Internal").ap()
        inv_d = nc.dram_tensor("inv_d", [HEADS, TOK], F32, kind="Internal").ap()
        g_d = nc.dram_tensor("g_d", [TOK, HID], F32, kind="Internal").ap()

        xs = sb("xs", [P, HALVES, KT, TOK], F16)
        att = sb("att", [P, KT, TOK], F32)
        qs = [sb(f"qs{i}", [P, HG, SEQ], BF16) for i in range(STEPS)]
        ks = [sb(f"ks{i}", [P, HG, SEQ], BF16) for i in range(STEPS)]
        va = [sb(f"va{b}", [P, QT, DT_HEADS, VC], F32) for b in range(BATCH)]
        probs = [sb(f"probs{i}", [P, HG, CH], F32) for i in range(3)]
        wqk = [sb(f"wqk{g}", [P, KT, P], F32) for g in range(2)]
        wv = sb("wv", [P, KT, P], F32)
        wqks = [sb(f"wqks{g}", [P, HALVES, KT, P], F16) for g in range(2)]
        wvs = sb("wvs", [P, HALVES, KT, P], F16)
        largest = sb("largest", [P, 8], F32)
        onesf = sb("onesf", [8, P], F32)
        diag = sb("diag", [8, 8], F32)
        bound = sb("bound", [P, 5], F32)
        power = sb("power", [P, 5], F32)
        inverse_p = sb("inverse_p", [P, 5], F32)
        scale = sb("scale", [P, 5], F32)
        back = sb("back", [P, 5], F32)
        back_proj = sb("back_proj", [P, 1], F32)
        bvs = sb("bvs", [P, KT], F32)
        ratio = sb("ratio", [P, 1], F32)
        ident16 = sb("ident16", [P, P], F16)
        bqk = [sb(f"bqk{g}", [P, 1], F32) for g in range(2)]
        qk = sb("qk", [P, SEQ], F32)
        pieces = sb("pieces", [P, PIECES, SEQ], BF16)
        raw = [sb(f"raw{c}", [P, CH], F32) for c in range(CHUNKS)]
        mask = sb("mask", [P, CH], F32)
        maskb = sb("maskb", [P, P], BF16)
        ident = sb("ident", [P, P], F32)
        identb = sb("identb", [P, P], BF16)
        junk = sb("junk", [P, 2, CH], BF16)
        tops = sb("tops", [P, CHUNKS, HG * QT], F32)
        top = sb("top", [P, HG * QT], F32)
        toprest = sb("toprest", [P, HG * QT], F32)
        negmax = sb("negmax", [P, PIECES, HG * QT], BF16)
        negmaxT = sb("negmaxT", [PIECES * HG * QT, P], BF16)
        bv = sb("bv", [P, KT], F32)
        stats = sb("stats", [P, 4, 6], F32)
        meanvar = sb("meanvar", [P, 4, 2], F32)
        std = sb("std", [P, 4], F32)
        rstd = sb("rstd", [P, 4], F32)
        small = sb("small", [P, 352], F32)
        bfb = sb("bfb", [P, HID], F32)

        def pb(name, shape):
            return ctx.enter_context(nc.psum_tensor(name, shape, F32))

        mxp = [pb(f"mxp{i}", [P, CH]) for i in range(2)]
        stp = [pb(f"stp{i}", [P, 2, CH]) for i in range(2)]
        accp = pb("accp", [P, CH])
        miscp = pb("miscp", [P, CH])
        ring = [stp[0][:, 0, :], stp[0][:, 1, :], stp[1][:, 0, :], stp[1][:, 1, :]]

        s_ident = sem("s_ident")
        s_const = sem("s_const")
        s_ones = sem("s_ones")
        s_x = [sem(f"s_x{i}") for i in range(5)]
        s_stats = sem("s_stats")
        s_var = sem("s_var")
        s_std = sem("s_std")
        s_rstd = sem("s_rstd")
        s_xn = sem("s_xn")
        s_xhi = sem("s_xhi")
        s_xlo = sem("s_xlo")
        s_watt = [sem(f"s_watt{i}") for i in range(2)]
        s_large = sem("s_large")
        s_col = sem("s_col")
        s_row = sem("s_row")
        s_scale = sem("s_scale")
        s_wscaled = sem("s_wscaled")
        s_whi = sem("s_whi")
        s_wlo = sem("s_wlo")
        s_xt = sem("s_xt")
        s_xte = sem("s_xte")
        s_lora = sem("s_lora")
        s_gsel = sem("s_gsel")
        s_lp = sem("s_lp")
        s_le = sem("s_le")
        s_bcat = sem("s_bcat")
        s_wf = sem("s_wf")
        s_ax = sem("s_ax")
        s_axe = sem("s_axe")
        s_ff = sem("s_ff")
        s_z = sem("s_z")
        s_g = sem("s_g")
        s_gst = [sem(f"s_gst{i}") for i in range(3)]
        s_w = [sem(f"s_w{g}") for g in range(2)]
        s_wv = sem("s_wv")
        s_misc = sem("s_misc")
        s_hi = sem("s_hi")
        s_v = sem("s_v")
        s_mid = sem("s_mid")
        s_rest = sem("s_rest")
        s_lo = sem("s_lo")
        s_stack = sem("s_stack")
        s_mx = sem("s_mx")
        s_mx_free = sem("s_mx_free")
        s_seen = sem("s_seen")
        s_top = sem("s_top")
        s_neg = sem("s_neg")
        s_negT = sem("s_negT")
        s_negrows = sem("s_negrows")
        s_scores = sem("s_scores")
        s_exp = sem("s_exp")
        s_pv = sem("s_pv")
        s_acc_free = sem("s_acc_free")
        s_raw = [sem(f"s_raw{c}") for c in range(CHUNKS)]
        s_sums = sem("s_sums")
        s_inv = sem("s_inv")
        s_invst = sem("s_invst")
        s_invb = [sem(f"s_invb{p}") for p in range(len(PARTS))]
        s_am = sem("s_am")
        s_as = sem("s_as")
        s_athi = sem("s_athi")
        s_lasthi = sem("s_lasthi")
        s_atlo = sem("s_atlo")
        s_last = sem("s_last")
        s_wpp = sem("s_wpp")
        s_wp = sem("s_wp")
        s_bp = sem("s_bp")
        s_xg = [sem(f"s_xg{i}") for i in range(4)]
        s_op = sem("s_op")
        s_y = sem("s_y")
        s_yg = sem("s_yg")
        s_res = sem("s_res")
        s_out = sem("s_out")

        def f32view(t):
            return t[:, :, :].rearrange("p a b -> p (a b)").bitcast(F32)

        xin = [*probs, va[1][:, :, :, :].rearrange("p a b c -> p (a b c)").rearrange("p (t d) -> p t d", t=4)]
        la = f32view(qs[1]).rearrange("p (k i) -> p k i", k=KT)
        lbr = f32view(ks[1]).rearrange("p (c m) -> p c m", c=KT)
        lbT = att[:, 2, :].rearrange("p (c m) -> p c m", c=KT)
        acat = att[:, 3, :].bitcast(F16).rearrange("p (a k g r) -> p a k g r", a=HALVES, k=KT, g=GROUPS)
        wfs = att[:, 1, :].bitcast(F16).rearrange("p (a k o) -> p a k o", a=HALVES, k=KT)
        watt = att[:, 0:3, :].rearrange("p a n -> p (a n)")
        xp = [t[:, :, :].rearrange("p a b -> p (a b)").bitcast(F16).rearrange("p (a t d) -> p a t d", a=HALVES, t=4)
              for t in (qs[2], qs[3], ks[2], ks[3])]
        axT = att[:, 0, :]
        va1 = va[1][:, :, :, :].rearrange("p a b c -> p (a b c)")
        gsel = va1[:, 0:KT * GROUPS * RANK]
        beff = va1[:, 1024:1024 + 2 * HID].rearrange("p (a o) -> p a o", a=2)
        bcat = [f32view(t)[0:RC, :].rearrange("p (g o) -> p g o", g=4) for t in (qs[3], ks[3])]
        wf = probs[0]
        las = raw[0][0:RANK, :]
        lbsT = raw[1][0:RANK, :]
        lbsr = small[:, 0:128].rearrange("p (c r) -> p c r", c=KT)
        pick = small[:, 128:160]
        gatep = small[:, 160:192]
        gateall = small[:, 192:320]
        z_t = raw
        g_t = [probs[1 + i // 4][:, i % 4, :] for i in range(8)]

        invb = [[f32view(t)[:, j * SEQ:(j + 1) * SEQ] for t in pair for j in range(2)]
                for pair in ((ks[0], qs[2]), (qs[1], ks[1]))]
        wp = f32view(qs[0]).rearrange("p (k o) -> p k o", k=KT)
        va_t = [t[:, :, :, :].rearrange("p a b c -> p (a b c)").rearrange("p (t d) -> p t d", t=4) for t in va]
        xt = [f32view(ks[2]).rearrange("p (t d) -> p t d", t=4), probs[0], probs[1], probs[2]]
        gt = [va_t[0], va_t[1], *(f32view(t).rearrange("p (t d) -> p t d", t=4) for t in (ks[3], qs[3]))]
        y_t = [t[:, :, :].rearrange("p k n -> p (k n)") for t in (wqk[1], wv)]
        atp = xs
        wpp = [t.rearrange("p (k o) -> p k o", k=KT)
               for t in (pieces[:, 0:2, :].rearrange("p a n -> p (a n)").bitcast(F16), qk[:, :].bitcast(F16))]
        flat = [t[:, :, :, :].rearrange("p a k n -> p (a k n)").bitcast(F32) for t in wqks]
        spare = wqk[0][:, :, :].rearrange("p k n -> p (k n)")
        sums = [flat[0][0:96, 0:256], flat[0][:, 256:512], spare[:, 0:64]]
        inv = [flat[1][0:96, 0:256], flat[1][:, 256:512], spare[:, 64:128]]

        block = ctx.enter_context(nc.Block())

        def dt_of(trip, ahead):
            return trip + ahead // STEPS

        def repeated(a, at, n):
            return bass.AP(tensor=a.tensor, offset=a.offset, ap=[*a.ap[:at], [0, n], *a.ap[at:]])

        def row(a):
            return bass.AP(tensor=a.tensor, offset=a.offset, ap=[[0, P], [1, HID]])

        @block.sync
        def _(sp):
            def load_x(i, lo, hi, sem):
                sp.dma_start(xin[i][:, lo:hi, :],
                             x[(4 * i + lo) * P:(4 * i + hi) * P, :].rearrange("(t p) d -> p t d", p=P))\
                  .then_inc(sem, 16)

            def load_wqk(g, dt):
                sp.dma_start(wqk[g][:, :, :], w_qk[bass.ds(dt * 2 + g, 1)].rearrange("g (k p) n -> p (g k) n", p=P))\
                  .then_inc(s_w[g], 16)
                sp.dma_start(bqk[g][:, :], b_qk[bass.ds(dt * 2 + g, 1)].rearrange("g p -> p g"),
                             allow_slow_non_contiguous=True).then_inc(s_w[g], 16)

            def load_wv(dt):
                sp.dma_start(wv[:, :, :], w_v.rearrange("(k p) n -> p k n", p=P)[:, :, bass.ds(dt * P, P)])\
                  .then_inc(s_wv, 16)

            load_x(0, 0, 2, s_x[0])
            load_x(0, 2, 4, s_x[4])
            sp.dma_start(ident[:, :], ident_d).then_inc(s_ident, 16)
            sp.dma_start(ident16[:, :], ident16_d).then_inc(s_ident, 16)
            load_x(1, 0, 4, s_x[1])
            sp.dma_start(watt[:, 0:4 * SEQ].rearrange("p (g k n) -> p g k n", g=2 * DTS, k=KT)
                         .rearrange("p g k n -> p (g k) n"),
                         w_qk.rearrange("g (k p) n -> p (g k) n", p=P)).then_inc(s_watt[0], 16)
            sp.dma_start(watt[:, 4 * SEQ:6 * SEQ].rearrange("p (k n) -> p k n", k=KT),
                         w_v.rearrange("(k p) n -> p k n", p=P)).then_inc(s_watt[1], 16)
            load_wqk(0, 0)
            load_wv(0)
            load_x(2, 0, 4, s_x[2])
            load_x(3, 0, 4, s_x[3])
            load_wqk(1, 0)
            for tile, src in ((pick, pick_d), (gateall, bass.AP(tensor=gate.tensor, offset=gate.offset,
                                                                ap=[[0, P], [1, GROUPS * LORAS]])),
                              (la, lora_a.rearrange("n r i -> (n r) i").rearrange("(k p) i -> p k i", p=P)),
                              (las[:, :], lora_as), (lbsr, lora_bs.rearrange("(c p) r -> p c r", p=P))):
                sp.dma_start(tile, src).then_inc(s_lora, 16)
            for c in range(KT):
                sp.dma_start(lbr.rearrange("p c (n r) -> p c n r", r=RANK)[:, c],
                             lora_b[:, c * P:(c + 1) * P, :].rearrange("n o r -> o n r")).then_inc(s_lora, 16)
            for t in (qs[0], ks[0]):
                sp.dma_start(t[ALIBI0:ROWS_ALL, :, :], ones_d).then_inc(s_ones, 16)
            sp.wait_ge(s_xlo, 4)
            sp.dma_start(wf[:, :, :], w_ffn.rearrange("(k p) o -> p k o", p=P)).then_inc(s_wf, 16)
            sp.dma_start(bfb[:, :], row(b_ffn)).then_inc(s_wf, 16)
            for tile, src in ((identb, identb_d), (mask, mask_d), (maskb, maskb_d), (bv, b_v)):
                sp.dma_start(tile[:, :], src).then_inc(s_const, 16)

            pieced = Tally()
            negs = Tally()
            vs = Tally()
            accs = Tally()

            def stack(trip, ahead):
                u = ahead % STEPS
                pieced.add()
                sp.wait_ge(s_hi, pieced.at(trip, STEPS) * CHUNKS)
                sp.wait_ge(s_lo, pieced.at(trip, STEPS))
                for a, (tile, order) in enumerate(((qs[u], Q_PIECES), (ks[u], K_PIECES))):
                    for r, piece in enumerate(order):
                        sp.dma_start(tile[r * HD:(r + 1) * HD, :, :],
                                     pieces[a * 64:(a + 1) * 64, piece, :]).then_inc(s_stack, 16)
                group = 2 * dt_of(trip, ahead) + u % 2
                sp.dma_start(ks[u][ALIBI0:ALIBI0 + PIECES, :, :].rearrange("p h n -> p (h n)"),
                             alibi_d[bass.ds(group, 1)].rearrange("g p n -> (g p) n")).then_inc(s_stack, 16)

            def neg_rows(trip, ahead):
                u = ahead % STEPS
                negs.add()
                sp.wait_ge(s_negT, negs.at(trip, STEPS))
                sp.dma_start(qs[u][NEGMAX0:ROWS_ALL, :, :], negmaxT[:, :]).then_inc(s_negrows, 16)

            def store_raw(trip, u, c):
                accs.add()
                dt = dt_of(trip, u)
                g, b = u % 2, u // 2
                sp.wait_ge(s_acc_free, accs.at(trip, CHUNKS * STEPS) + 1)
                at = b * SEQ + c * CH
                sp.dma_start(att[g * 64:(g + 1) * 64, bass.ds(dt, 1), at:at + CH],
                             raw[c][0:P:2, :]).then_inc(s_raw[c], 16)
                sp.dma_start(sums_d[bass.ds(dt * DT_HEADS + g * HG, HG), at:at + CH],
                             raw[c][1:P:VC, :]).then_inc(s_raw[c], 16)

            sp.wait_ge(s_ones, 16 * 2)
            stack(0, 0)
            sp.wait_ge(s_xt, NT)
            sp.wait_ge(s_lp, 2 * KT)
            for t in (*qs[1:], *ks[1:]):
                sp.dma_start(t[ALIBI0:ROWS_ALL, :, :], ones_d).then_inc(s_ones, 16)
            sp.wait_ge(s_ones, 16 * 2 * STEPS)
            sp.wait_ge(s_le, 12)
            for g in range(GROUPS):
                sp.dma_start(bcat[g // 4][0:RANK, g % 4, :], beff[(g % 4) * RANK:(g % 4 + 1) * RANK, g // 4, :])\
                  .then_inc(s_bcat, 16)
            for t in bcat:
                sp.dma_start(t[RANK:RC, :, :], repeated(lbsT, 1, 4)).then_inc(s_bcat, 16)
            stack(0, 1)
            stack(0, 2)
            neg_rows(0, 0)
            vs.add(2)
            for c in range(CHUNKS):
                sp.sem_inc(s_raw[c], 32)

            def step(trip, u, last):
                plan = Plan(u, last)
                if not last and u < 2:
                    load_wqk(u, dt_of(trip, STEPS))
                if not last and u == 2:
                    sp.wait_ge(s_v, vs.at(trip, STEPS))
                    load_wv(dt_of(trip, STEPS))
                if plan.v:
                    vs.add()
                store_raw(trip, u, 0)
                if plan.neg:
                    neg_rows(trip, u + 1)
                if plan.qk:
                    stack(trip, u + 3)

            with sp.Fori(0, DTS - 1, 1) as trip:
                for u in range(STEPS):
                    step(trip, u, False)
                    store_raw(trip, u, 1)
            more = DTS - 2
            for t in (pieced, negs, vs):
                t.n += STEPS * more
            accs.n += CHUNKS * STEPS * more

            def stretches(t, p):
                b, dts = PARTS[p]
                return t[dts[0] * DT_HEADS:(dts[-1] + 1) * DT_HEADS, b * SEQ:(b + 1) * SEQ]\
                    .rearrange("h (a n) -> h a n", n=64 if len(dts) == 1 else 256)

            def sums_in(p, steps):
                for c in range(CHUNKS):
                    sp.wait_ge(s_raw[c], 32 * (1 + STEPS * (DTS - 1) + steps))
                sp.dma_start(sums[p], stretches(sums_d, p)).then_inc(s_sums, 16)

            def store_inverses(p):
                sp.wait_ge(s_inv, p + 1)
                sp.dma_start(stretches(inv_d, p), inv[p]).then_inc(s_invst, 16)

            def inverses(p):
                sp.wait_ge(s_invst, 16 * (p + 1))
                b, dts = PARTS[p]
                for dt in dts:
                    src = inv_d[dt * DT_HEADS:(dt + 1) * DT_HEADS, b * SEQ:(b + 1) * SEQ]
                    sp.dma_start(invb[b][dt], bass.AP(tensor=src.tensor, offset=src.offset,
                                                      ap=[[TOK, DT_HEADS], [0, HD], [1, SEQ]])).then_inc(s_invb[p], 16)

            def load_xg(i):
                rows = slice(i * 4 * P, (i + 1) * 4 * P)
                sp.dma_start(xt[i][:, :, :], x[rows, :].rearrange("(t p) d -> p t d", p=P)).then_inc(s_xg[i], 16)
                sp.dma_start(gt[i][:, :, :], g_d[rows, :].rearrange("(t p) d -> p t d", p=P)).then_inc(s_xg[i], 16)

            for u in range(STEPS):
                if u == 1:
                    sums_in(0, 0)
                if u == 2:
                    sums_in(1, 2)
                step(DTS - 1, u, True)
                if u == 1:
                    store_inverses(0)
                if u == 2:
                    store_inverses(1)
                store_raw(DTS - 1, u, 1)
                if u == 0:
                    sp.dma_start(wp, w_proj.rearrange("(k p) o -> p k o", p=P)).then_inc(s_wp, 16)
                if u == 1:
                    inverses(0)
                if u == 2:
                    inverses(1)
                    sp.wait_ge(s_z, NT)
                    sp.dma_start(bfb[:, :], row(b_proj)).then_inc(s_bp, 16)
                    for i, tiles in enumerate((8, 4, 4)):
                        sp.wait_ge(s_gst[i], 16 * tiles)
                    load_xg(0)
            sums_in(2, 4)
            store_inverses(2)
            inverses(2)
            for i in range(1, 4):
                load_xg(i)
            for i in range(NT):
                sp.wait_ge(s_res, i + 1)
                sp.dma_start(out[i * P:(i + 1) * P, :], xt[i // 4][:, i % 4, :]).then_inc(s_out, 16)
            sp.wait_ge(s_out, 16 * NT)

        @block.tensor
        def _(pe):
            def transposes(i):
                for t in range(4):
                    n = 4 * i + t
                    pe.wait_ge(s_xlo, n + 1)
                    if n >= 4:
                        pe.wait_ge(s_xte, n - 3)
                    for a in range(HALVES):
                        for k in range(KT):
                            o = (a * KT + k) * P
                            m = pe.transpose(ring[n % 4].bitcast(F16)[:, o:o + P], xp[i][:, a, t, k * P:(k + 1) * P],
                                             ident16[:, :])
                    m.then_inc(s_xt, 1)

            def in_row(n, i):
                pe.wait_ge(s_col, 2 * i + 1)
                pe.transpose(mxp[i % 2][0:n, 0:P], largest[:, 0:n], ident[:, :]).then_inc(s_row, 1)

            def on_all(n, i):
                pe.wait_ge(s_col, 2 * i + 2)
                pe.matmul(mxp[i % 2][:, P:P + n], onesf[0:n, :], diag[0:n, 0:n], start=True, stop=True).then_inc(s_row, 1)

            def lora_prep(between):
                uses = Tally()

                def bank():
                    if uses.n >= 4:
                        pe.wait_ge(s_le, uses.n - 3)
                    uses.add()
                    return ring[(uses.n - 1) % 4]

                pe.wait_ge(s_lora, 16 * 9)
                for k in range(KT):
                    b = bank()
                    for c in range(KT):
                        m = pe.transpose(b[:, c * P:(c + 1) * P], lbr[:, c, k * P:(k + 1) * P], ident[:, :])
                    m.then_inc(s_lp, 1)
                pe.wait_ge(s_gsel, 2)
                for it in range(KT):
                    b = bank()
                    for k in range(KT):
                        m = pe.matmul(b[:, 0:GROUPS * RANK], la[:, k, it * P:(it + 1) * P],
                                      gsel[:, k * 256:(k + 1) * 256], start=(k == 0), stop=(k == KT - 1))
                    m.then_inc(s_lp, 1)
                b = bank()
                for c in range(KT):
                    m = pe.transpose(b[0:RANK, c * P:(c + 1) * P], lbsr[:, c, :], ident[:, :])
                m.then_inc(s_lp, 1)
                b = bank()
                for it in range(KT):
                    m = pe.transpose(b[:, it * RANK:(it + 1) * RANK], las[:, it * P:(it + 1) * P], ident[0:RANK, 0:RANK])
                m.then_inc(s_lp, 1)
                for half in range(2):
                    if half == 1:
                        between()
                    b = bank()
                    if half == 0:
                        pe.wait_ge(s_le, KT)
                    for k in range(KT):
                        m = pe.matmul(b[:, :], gsel[:, k * 256 + half * P:k * 256 + (half + 1) * P], lbT[:, k, :],
                                      start=(k == 0), stop=(k == KT - 1))
                    m.then_inc(s_lp, 1)

            qks, vs, negTs = Tally(), Tally(), Tally()
            splits = Tally()
            stacked = Tally()
            maxed = Tally()
            negd = Tally()
            negrows = Tally()
            pairs = Tally()
            chunks = Tally()
            exps = Tally()
            held = []

            def misc_free(trip):
                if held:
                    s, tally, rate = held[-1]
                    pe.wait_ge(s, tally.at(trip, rate))

            def misc_used(ins, s, tally, rate):
                ins.then_inc(s_misc, 1)
                tally.add()
                held.append((s, tally, rate))

            def qk_part(trip, ahead, c, k):
                u = ahead % STEPS
                g, b = u % 2, u // 2
                if k == 0:
                    misc_free(trip)
                    if c == 0 and b == 0:
                        splits.add()
                        pe.wait_ge(s_wlo, splits.at(trip, 3))
                for wa, xa in PASSES:
                    m = pe.matmul(miscp[:, :], wqks[g][:, wa, k, :],
                                  xs[:, xa, k, b * SEQ + c * CH:b * SEQ + (c + 1) * CH],
                                  start=(k == 0 and (wa, xa) == PASSES[0]),
                                  stop=(k == KT - 1 and (wa, xa) == PASSES[-1]))
                if k == KT - 1:
                    misc_used(m, s_hi, qks, CHUNKS * STEPS)

            def v_part(trip, b, half, t):
                if t == 0:
                    misc_free(trip)
                    if half == 0 and b == 0:
                        splits.add()
                        pe.wait_ge(s_wlo, splits.at(trip, 3))
                tt = b * QT + half * 4 + t
                for k in range(KT):
                    for wa, xa in PASSES:
                        m = pe.matmul(miscp[:, t * P:(t + 1) * P], xs[:, xa, k, tt * P:(tt + 1) * P], wvs[:, wa, k, :],
                                      start=(k == 0 and (wa, xa) == PASSES[0]),
                                      stop=(k == KT - 1 and (wa, xa) == PASSES[-1]))
                if t == 3:
                    misc_used(m, s_v, vs, STEPS)

            def max_part(trip, ahead, i):
                u = ahead % STEPS
                h, t, c = MAXES[i]
                if i == 0:
                    stacked.add(16 * 13)
                    pe.wait_ge(s_stack, stacked.at(trip, 16 * 13 * STEPS))
                if maxed.n >= 2:
                    pe.wait_ge(s_mx_free, maxed.at(trip, NM * STEPS, 1))
                w = keys_of(t, c)
                pe.matmul(mxp[maxed.n % 2][:, 0:w], qs[u][0:ROWS_MAX, h, t * P:(t + 1) * P],
                          ks[u][0:ROWS_MAX, h, c * CH:c * CH + w], start=True, stop=True).then_inc(s_mx, 1)
                maxed.add()

            def neg_part(trip):
                misc_free(trip)
                negd.add()
                pe.wait_ge(s_neg, negd.at(trip, STEPS))
                m = pe.matmul(miscp[0:PIECES * HG * QT, 0:P], negmax[:, :, :].rearrange("p a b -> p (a b)"),
                              identb[:, :], start=True, stop=True)
                misc_used(m, s_negT, negTs, STEPS)

            def score_part(trip, u, n, pair):
                c, kb = UNITS[n]
                w = width(n)
                if n == 0 and pair == 0:
                    negrows.add(16)
                    pe.wait_ge(s_negrows, negrows.at(trip, 16 * STEPS))
                pe.wait_ge(s_exp, pairs.at(trip, 2 * NU * STEPS) + 1)
                for j in range(2):
                    h = 2 * pair + j
                    to = stp[pairs.n % 2][:, j, :]
                    m = pe.matmul(to[:, 0:w], ks[u][0:ROWS_ALL, h, kb * P:(kb + 1) * P],
                                  qs[u][0:ROWS_ALL, h, (c + 1) * CH - w:(c + 1) * CH], start=True,
                                  stop=not diagonal(n))
                    if diagonal(n):
                        m = pe.matmul(to[:, 0:P], identb[:, :], maskb[:, :], start=False, stop=True)
                m.then_inc(s_scores, 1)
                pairs.add()

            def pv_part(trip, u, n):
                c, kb = UNITS[n]
                w = width(n)
                g, b = u % 2, u // 2
                exps.add(2)
                pe.wait_ge(s_exp, exps.at(trip, 2 * NU * STEPS) + 2)
                if kb == 0:
                    chunks.add()
                    pe.wait_ge(s_acc_free, chunks.at(trip, CHUNKS * STEPS))
                for h in range(HG):
                    m = pe.matmul(accp[VC * h:VC * (h + 1), CH - w:CH], va[b][:, kb, g * HG + h, :],
                                  probs[(exps.n // 2 - 1) % 3][:, h, 0:w], start=(kb == 0),
                                  stop=(n == NU - 1 or UNITS[n + 1][0] != c))
                m.then_inc(s_pv, 1)

            pe.wait_ge(s_ident, 32)
            def qk_all(ahead, c):
                for k in range(KT):
                    qk_part(0, ahead, c, k)

            def v_all(half):
                for t in range(4):
                    v_part(0, 0, half, t)

            transposes(0)
            transposes(1)
            in_row(2, 0)
            on_all(2, 0)
            pe.wait_ge(s_xte, 8)
            qk_all(0, 0)
            transposes(2)
            qk_all(0, 1)
            v_all(0)
            transposes(3)
            in_row(4, 1)
            for t in range(4):
                v_part(0, 0, 1, t)
                if t == 1:
                    on_all(4, 1)
            qk_all(1, 0)
            pe.wait_ge(s_xte, NT)
            lora_prep(lambda: qk_all(1, 1))
            pe.wait_ge(s_le, 12)
            for i in range(4):
                for j in range(2):
                    g = 2 * i + j
                    for k in range(KT):
                        for aa, xa in PASSES:
                            m = pe.matmul(ring[i][0:RC, j * GTOK:(j + 1) * GTOK], acat[:, aa, k, g, :],
                                          xs[:, xa, k, g * GTOK:(g + 1) * GTOK],
                                          start=(k == 0 and (aa, xa) == PASSES[0]),
                                          stop=(k == KT - 1 and (aa, xa) == PASSES[-1]))
                m.then_inc(s_ax, 1)
            pe.wait_ge(s_const, 16 * 4)
            splits.add()
            pe.wait_ge(s_wlo, splits.n)
            pe.wait_ge(s_bcat, 16 * (GROUPS + 2))
            todo = list(FIRST_MAXES)
            for i in range(NT):
                g = i * P // GTOK
                if i == 0:
                    pe.wait_ge(s_axe, 4)
                if i >= 4:
                    pe.wait_ge(s_z, i - 3)
                for k in range(KT + 1):
                    if k < KT:
                        for wa, xa in PASSES:
                            m = pe.matmul(ring[i % 4], xs[:, xa, k, i * P:(i + 1) * P], wfs[:, wa, k, :],
                                          start=(k == 0 and (wa, xa) == PASSES[0]), stop=False)
                    else:
                        m = pe.matmul(ring[i % 4], axT[0:RC, i * P:(i + 1) * P], bcat[g // 4][:, g % 4, :],
                                      start=False, stop=True)
                    if todo:
                        max_part(0, *todo.pop(0))
                m.then_inc(s_ff, 1)
                if i in QK_AT:
                    qk_all(2, QK_AT.index(i))
                if i == NEG_AT + 1:
                    neg_part(0)
            assert not todo
            pe.sem_inc(s_pv, 3)
            for pair in range(2):
                pe.wait_ge(s_z, NT - 2 + 2 * pair)
                score_part(0, 0, 0, pair)

            def fill(trip, u, n, plan):
                for what, *at in FILL.get(n, ()):
                    if what == "qk" and plan.qk:
                        qk_part(trip, u + 3, *at)
                    if what == "neg" and plan.neg:
                        neg_part(trip)
                    if what == "v" and plan.v:
                        v_part(trip, (u // 2 + 1) % 2, u % 2, *at)

            held.append((s_v, vs, STEPS))

            def step(trip, u, last):
                plan = Plan(u, last)
                for n in range(NU):
                    todo = maxes_of(n, plan.near, plan.far)
                    for pair in range(2):
                        if n < NU - 1:
                            score_part(trip, u, n + 1, pair)
                        elif plan.neg:
                            score_part(trip, (u + 1) % STEPS, 0, pair)
                        if todo:
                            max_part(trip, u + todo[0][0], todo.pop(0)[1])
                    if n not in LATE:
                        fill(trip, u, n, plan)
                    if n in FILL and n not in LATE and todo:
                        max_part(trip, u + todo[0][0], todo.pop(0)[1])
                    pv_part(trip, u, n)
                    if last and u == 2 and n == HALF_U:
                        in_row(1, 2)
                    if last and u == 2 and n == HALF_U + 1:
                        on_all(1, 2)
                    if todo:
                        max_part(trip, u + todo[0][0], todo.pop(0)[1])
                    if n in LATE:
                        fill(trip, u, n, plan)
                    while todo:
                        max_part(trip, u + todo[0][0], todo.pop(0)[1])

            with pe.Fori(0, DTS - 1, 1) as trip:
                for u in range(STEPS):
                    step(trip, u, False)
            more = DTS - 2
            qks.n += CHUNKS * STEPS * more
            for t in (vs, negTs, negd):
                t.n += STEPS * more
            splits.n += 3 * more
            stacked.n += 16 * 13 * STEPS * more
            maxed.n += NM * STEPS * more
            pairs.n += 2 * NU * STEPS * more
            exps.n += 2 * NU * STEPS * more
            chunks.n += CHUNKS * STEPS * more
            negrows.n += 16 * STEPS * more
            for u in range(STEPS):
                step(DTS - 1, u, True)

            pe.wait_ge(s_exp, 2 + pairs.n)
            pe.wait_ge(s_wpp, 1)
            for i in range(NT):
                if i >= 4:
                    pe.wait_ge(s_y, i - 3)
                for k in range(KT):
                    if i == 0:
                        pe.wait_ge(s_atlo, DTS + k)
                    if i == NT // BATCH and k == KT - 1:
                        pe.wait_ge(s_last, 1)
                    for wa, xa in PASSES:
                        m = pe.matmul(ring[i % 4], atp[:, xa, k, i * P:(i + 1) * P], wpp[wa][:, k, :],
                                      start=(k == 0 and (wa, xa) == PASSES[0]),
                                      stop=(k == KT - 1 and (wa, xa) == PASSES[-1]))
                m.then_inc(s_op, 1)

        @block.scalar
        def _(act):
            def roots(i):
                act.wait_ge(s_var, i + 1)
                act.activation(std[:, :], meanvar[:, :, 1], ACT.Sqrt, scale=1 / X_SCALE ** 2).then_inc(s_std, 1)

            def first_pieces(i):
                for t in range(4):
                    act.wait_ge(s_xn, 4 * i + t + 1)
                    act.activation(xp[i][:, 0, t, :], xin[i][:, t, :], ACT.Copy).then_inc(s_xhi, 1)

            scalings = Tally()

            def weights_out(trip, pieces_t, whole, weight_scale, s, count):
                flat = whole[:, :, :].rearrange("p k n -> p (k n)")
                act.wait_ge(s, count)
                act.activation(flat, flat, ACT.Identity, scale=weight_scale).then_inc(s_wscaled, 1)
                scalings.add()
                act.wait_ge(s_wscaled, scalings.at(trip, 3))
                act.activation(pieces_t[:, 0].rearrange("p k n -> p (k n)"), flat, ACT.Copy).then_inc(s_whi, 1)

            def transposed(i):
                for t in range(4):
                    n = 4 * i + t
                    act.wait_ge(s_xt, n + 1)
                    act.activation(xs[:, :, :, n * P:(n + 1) * P].rearrange("p a k n -> p (a k) n"),
                                   ring[n % 4].bitcast(F16).rearrange("p (b m) -> p b m", m=P), ACT.Copy)\
                       .then_inc(s_xte, 1)

            miscs = Tally()
            stacked = Tally()
            pairs = Tally()
            used = Tally()
            negs = Tally()
            RM = (CHUNKS + 2) * STEPS

            def misc_full(trip):
                miscs.add()
                act.wait_ge(s_misc, miscs.at(trip, RM))

            def qk_out(trip, ahead, c):
                g = ahead % 2
                if c == 0 and stacked.n:
                    act.wait_ge(s_stack, stacked.at(trip, 16 * 13 * STEPS))
                misc_full(trip)
                part = slice(c * CH, (c + 1) * CH)
                act.activation(qk[:, part], miscp[:, :], ACT.Identity, bias=bqk[g][:, 0:1], scale=back[:, 0:1])
                act.activation(pieces[:, 0, part], miscp[:, :], ACT.Identity, bias=bqk[g][:, 0:1],
                               scale=back[:, 0:1]).then_inc(s_hi, 1)
                if c == 1:
                    stacked.add(16 * 13)

            def v_out(trip, b, half):
                misc_full(trip)
                act.activation(va[b][:, half * 4:(half + 1) * 4, :, :].rearrange("p t h (d e) -> p (t h d) e", e=2)[:, :, 0],
                               miscp[:, :], ACT.Identity, scale=back[:, 0:1]).then_inc(s_v, 1)

            def neg_out(trip):
                misc_full(trip)
                if negs.n:
                    act.wait_ge(s_negrows, negs.at(trip, 16 * STEPS))
                act.activation(negmaxT[:, :], miscp[0:PIECES * HG * QT, 0:P], ACT.Copy).then_inc(s_negT, 1)
                negs.add(16)

            wloads = [Tally(), Tally()]
            vloads = Tally()

            def wqk_out(trip, g):
                wloads[g].add(32)
                weights_out(trip, wqks[g], wqk[g], scale[:, 0:1], s_w[g], wloads[g].at(trip, 32))

            def wv_out(trip):
                vloads.add(16)
                weights_out(trip, wvs, wv, scale[:, 0:1], s_wv, vloads.at(trip, 16))

            roots(0)
            first_pieces(0)
            roots(1)
            transposed(0)
            first_pieces(1)
            transposed(1)
            act.wait_ge(s_scale, 1)
            wqk_out(0, 0)
            wv_out(0)
            roots(2)
            wqk_out(0, 1)
            first_pieces(2)
            qk_out(0, 0, 0)
            roots(3)
            transposed(2)
            qk_out(0, 0, 1)
            first_pieces(3)
            v_out(0, 0, 0)
            transposed(3)
            v_out(0, 0, 1)
            act.wait_ge(s_scale, 2)
            weights_out(0, wfs, wf, scale[:, 1:2], s_wf, 32)
            for c in range(CHUNKS):
                qk_out(0, 1, c)
            for i in range(4):
                act.wait_ge(s_ax, i + 1)
                act.activation(axT[0:RC, i * CH:(i + 1) * CH], ring[i][0:RC, :], ACT.Identity,
                               scale=ratio[0:RC, :]).then_inc(s_axe, 1)
            act.sem_inc(s_exp, 2)
            for i in range(NT):
                act.wait_ge(s_z, i + 1)
                if i == 8:
                    act.wait_ge(s_gst[0], 16 * 8)
                act.activation(g_t[i % 8], z_t[i % 2][:, :], ACT.Silu).then_inc(s_g, 1)
                act.wait_ge(s_g, i + 1)
                act.dma_start(g_d[i * P:(i + 1) * P, :], g_t[i % 8]).then_inc(s_gst[max(0, i // 4 - 1)], 16)
                if i in QK_AT:
                    qk_out(0, 2, QK_AT.index(i))
                if i == NEG_AT + 1:
                    neg_out(0)

            def step(trip, u, last):
                plan = Plan(u, last)
                for n in range(NU):
                    w = width(n)
                    buf = probs[used.n % 3]
                    act.wait_ge(s_pv, used.at(trip, NU * STEPS) + 1)
                    for pair in range(2):
                        i = pairs.n
                        pairs.add()
                        act.wait_ge(s_scores, pairs.at(trip, 2 * NU * STEPS))
                        act.activation(buf[:, 2 * pair:2 * pair + 2, 0:w], stp[i % 2][:, :, 0:w], ACT.Exp,
                                       scale=SCALE).then_inc(s_exp, 1)
                    used.add()
                    if u == 0 and n < 2:
                        act.wait_ge(s_gst[1 + n], 16 * 4)
                    if n == WEIGHTS_AT and not last and u < 2:
                        wqk_out(trip, u)
                    if n == WEIGHTS_AT and not last and u == 2:
                        wv_out(trip)
                    what, *at = EMPTY.get(n, ("",))
                    if what == "qk" and plan.qk:
                        qk_out(trip, u + 3, *at)
                    if what == "neg" and plan.neg:
                        neg_out(trip)
                    if what == "v" and plan.v:
                        v_out(trip, (u // 2 + 1) % 2, u % 2)

            with act.Fori(0, DTS - 1, 1) as trip:
                for u in range(STEPS):
                    step(trip, u, False)
            more = DTS - 2
            for t in wloads:
                t.n += 32 * more
            vloads.n += 16 * more
            scalings.n += 3 * more
            miscs.n += RM * more
            stacked.n += 16 * 13 * STEPS * more
            pairs.n += 2 * NU * STEPS * more
            used.n += NU * STEPS * more
            negs.n += 16 * STEPS * more
            for u in range(STEPS):
                step(DTS - 1, u, True)
            act.wait_ge(s_as, 2 * DTS)
            act.activation(atp[:, 0, DTS - 1, SEQ:2 * SEQ], att[:, DTS - 1, SEQ:2 * SEQ], ACT.Copy).then_inc(s_lasthi, 1)

        @block.vector
        def _(dve):
            larges = Tally()

            def link_large():
                larges.add()
                dve.wait_ge(s_large, larges.n)

            def largest_to(col, t, parts=P):
                dve.tensor_reduce(largest[0:parts, col:col + 1], t, AX.X, ALU.max, apply_absolute_value=True)\
                   .then_inc(s_large, 1)
                link_large()

            def over_all(n, i):
                dve.sem_inc(s_col, 1)
                over_row(n, i)
                dve.wait_ge(s_row, 2 * i + 2)

            def over_row(n, i):
                dve.wait_ge(s_row, 2 * i + 1)
                dve.tensor_reduce(largest[0:n, 7:8], mxp[i % 2][0:n, 0:P], AX.X, ALU.max).then_inc(s_large, 1)
                link_large()
                dve.tensor_scalar(diag[0:n, 0:n], ident[0:n, 0:n], largest[0:n, 7:8], None, ALU.mult).then_inc(s_col, 1)

            def scales(lo, hi):
                e, r = power[:, lo:hi], inverse_p[:, lo:hi]
                dve.tensor_scalar(bound[:, lo:hi], bound[:, lo:hi], SMALLEST, None, ALU.max).then_inc(s_large, 1)
                link_large()
                dve.tensor_scalar(e.bitcast(I32), bound[:, lo:hi].bitcast(I32), EXPONENT, None, ALU.bitwise_and)\
                   .then_inc(s_large, 1)
                link_large()
                dve.reciprocal(r, e).then_inc(s_large, 1)
                link_large()
                dve.tensor_scalar(r, r, 1 + 2.0 ** -10, None, ALU.mult).then_inc(s_large, 1)
                link_large()
                dve.tensor_scalar(r.bitcast(I32), r.bitcast(I32), EXPONENT, None, ALU.bitwise_and).then_inc(s_large, 1)
                link_large()
                dve.tensor_scalar(back[:, lo:hi], e, 1 / (W_SCALE * X_SCALE), None, ALU.mult)
                dve.tensor_scalar(scale[:, lo:hi], r, W_SCALE, None, ALU.mult).then_inc(s_scale, 1)

            for i in range(4):
                dve.wait_ge(s_x[i], 16)
                for t in range(4):
                    if i == 0 and t == 2:
                        dve.wait_ge(s_x[4], 16)
                    dve.bn_stats(stats[:, t, :], xin[i][:, t, :]).then_inc(s_stats, 1)
                dve.wait_ge(s_stats, 5 * i + 4)
                for t in range(4):
                    m = dve.bn_aggr(meanvar[:, t, :], stats[:, t, :])
                m.then_inc(s_stats, 1)
                dve.wait_ge(s_stats, 5 * i + 5)
                dve.tensor_scalar(meanvar[:, :, 1], meanvar[:, :, 1], EPS, None, ALU.add).then_inc(s_var, 1)
                dve.wait_ge(s_std, i + 1)
                dve.reciprocal(rstd[:, :], std[:, :]).then_inc(s_rstd, 1)
                dve.wait_ge(s_rstd, i + 1)
                for t in range(4):
                    dve.tensor_scalar(xin[i][:, t, :], xin[i][:, t, :], meanvar[:, t, 0:1], rstd[:, t:t + 1],
                                      ALU.subtract, ALU.mult).then_inc(s_xn, 1)
                if i == 0:
                    dve.memset(onesf[:, :], 1.0)
                if i == 1:
                    for part, (lo, hi) in enumerate(((0, 4 * SEQ), (4 * SEQ, 6 * SEQ))):
                        dve.wait_ge(s_watt[part], 16)
                        largest_to(part, watt[:, lo:hi])
                    over_all(2, 0)
                    dve.tensor_reduce(bound[:, 0:1], mxp[0][:, P:P + 2], AX.X, ALU.max).then_inc(s_large, 1)
                    link_large()
                    scales(0, 1)
                if i == 3:
                    dve.memset(va[0][:, :, :, :].rearrange("p t h (d e) -> p (t h d) e", e=2)[:, :, 1], 1.0)
                    dve.memset(tops[:, :, :], NEG)

            dve.wait_ge(s_lora, 16 * 9)
            dve.wait_ge(s_const, 16 * 4)
            dve.wait_ge(s_lora, 16 * 9)
            dve.wait_ge(s_wf, 32)
            dve.memset(largest[:, 2:3], 0.0)
            largest_to(0, wf[:, :, :].rearrange("p k o -> p (k o)"))
            largest_to(1, la.rearrange("p k i -> p (k i)"))
            largest_to(2, las[:, :], RANK)
            largest_to(3, bv[:, :])
            largest_to(4, gateall)
            over_all(4, 1)
            dve.tensor_copy(bound[:, 1:2], mxp[1][:, P:P + 1])
            dve.tensor_scalar(bound[:, 2:3], mxp[1][:, P + 1:P + 2], largest[:, 4:5], float(LORAS), ALU.mult, ALU.mult)\
               .then_inc(s_large, 1)
            link_large()
            dve.tensor_tensor(bound[:, 2:3], bound[:, 2:3], mxp[1][:, P + 2:P + 3], ALU.max).then_inc(s_large, 1)
            link_large()
            dve.tensor_scalar(bound[:, 3:4], bound[:, 0:1], float(HID), mxp[1][:, P + 3:P + 4], ALU.mult, ALU.add)\
               .then_inc(s_large, 1)
            link_large()
            scales(1, 4)
            dve.wait_ge(s_scale, 2)
            dve.tensor_scalar(bvs[:, :], bv[:, :], scale[:, 3:4], None, ALU.mult)
            dve.tensor_scalar(ratio[:, :], power[:, 2:3], inverse_p[:, 1:2], None, ALU.mult).then_inc(s_large, 1)
            for n in range(LORAS):
                k, p0 = n // 4, (n % 4) * RANK
                m = dve.tensor_copy(gatep[p0:p0 + RANK, k * GROUPS:(k + 1) * GROUPS],
                                     gateall[p0:p0 + RANK, n:GROUPS * LORAS:LORAS])
            m.then_inc(s_gsel, 1)
            dve.wait_ge(s_gsel, 1)
            dve.wait_ge(s_xlo, NT)
            dve.tensor_tensor(gsel.rearrange("p (g r) -> p g r", r=RANK), repeated(pick, 1, KT * GROUPS),
                              repeated(gatep, 2, RANK), ALU.mult).then_inc(s_gsel, 1)

            uses = Tally()

            def bank():
                uses.add()
                dve.wait_ge(s_lp, uses.n)
                return ring[(uses.n - 1) % 4]

            def pieces_of(to_hi, to_lo, what, hi_again):
                dve.tensor_scalar(to_hi, what, scale[:, 2:3], None, ALU.mult).then_inc(s_large, 1)
                link_large()
                return dve.scalar_tensor_tensor(out=to_lo, in0=what, scalar=scale[:, 2:3], in1=hi_again,
                                                op0=ALU.mult, op1=ALU.subtract)

            larges.add()
            for k in range(KT):
                dve.tensor_copy(lbT[:, k, :], bank()[:, :]).then_inc(s_le, 1)
            for it in range(KT):
                own = acat[:, :, it, :, 0:RANK]
                pieces_of(own[:, 0], own[:, 1], bank()[:, 0:256].rearrange("p (g r) -> p g r", g=GROUPS), own[:, 0])\
                    .then_inc(s_le, 1)
            dve.tensor_copy(lbsT[:, :], bank()[0:RANK, :]).then_inc(s_le, 1)
            b = bank()
            for k in range(KT):
                shared = acat[:, :, k, :, RANK:RC]
                m = pieces_of(shared[:, 0], shared[:, 1], repeated(b[:, k * RANK:(k + 1) * RANK], 1, GROUPS), shared[:, 0])
            m.then_inc(s_le, 1)
            for half in range(2):
                dve.tensor_copy(beff[:, half, :], bank()[:, :]).then_inc(s_le, 1)

            maxed = Tally()
            links = Tally()
            negs = Tally()
            pvs = Tally()
            rawd = Tally()

            def max_part(trip, i):
                h, t, c = MAXES[i]
                w = keys_of(t, c)
                bank = mxp[maxed.n % 2]
                maxed.add()
                dve.wait_ge(s_mx, maxed.at(trip, NM * STEPS))
                to = tops[:, c, h * QT + t:h * QT + t + 1]
                if t // CT == c:
                    dve.sem_inc(s_seen, 1)
                    m = dve.tensor_tensor_reduce(junk[:, (maxed.n - 1) % 2, 0:w], bank[:, 0:w], mask[:, CH - w:CH],
                                                 1.0, NEG, ALU.add, ALU.max, to)
                else:
                    m = dve.tensor_reduce(to, bank[:, 0:w], AX.X, ALU.max)
                m.then_inc(s_mx_free, 1)

            def neg_part(trip, link):
                if link == 0:
                    dve.wait_ge(s_mx_free, maxed.at(trip, NM * STEPS))
                    if negs.n:
                        dve.wait_ge(s_negT, negs.at(trip, STEPS))
                    negs.add()
                    ins = dve.tensor_tensor(top[:, :], tops[:, 0, :], tops[:, 1, :], ALU.max)
                else:
                    dve.wait_ge(s_top, links.at(trip, (LINKS - 1) * STEPS))
                if link == 1:
                    ins = dve.tensor_scalar(negmax[:, 0, :], top[:, :], -1.0, None, ALU.mult)
                if link == 2:
                    ins = dve.scalar_tensor_tensor(out=toprest[:, :], in0=top[:, :], scalar=-1.0,
                                                   in1=negmax[:, 0, :], op0=ALU.mult, op1=ALU.subtract)
                if link == 3:
                    ins = dve.tensor_copy(negmax[:, 1, :], toprest[:, :])
                if link < LINKS - 1:
                    ins.then_inc(s_top, 1)
                    links.add()
                else:
                    dve.tensor_tensor(negmax[:, 2, :], toprest[:, :], negmax[:, 1, :], ALU.subtract).then_inc(s_neg, 1)

            def acc_out(trip, c):
                pvs.add(CT * (c + 1))
                dve.wait_ge(s_pv, pvs.at(trip, NU * STEPS) + 3)
                if c == 0:
                    rawd.add(32)
                dve.wait_ge(s_raw[c], rawd.at(trip, 32 * STEPS))
                dve.tensor_copy(raw[c][:, :], accp[:, :]).then_inc(s_acc_free, 1)

            dve.wait_ge(s_const, 16 * 4)
            dve.wait_ge(s_wf, 32)
            todo = list(FIRST_MAXES)

            def z_out(i):
                dve.wait_ge(s_ff, i + 1)
                if i >= 2:
                    dve.wait_ge(s_g, i - 1)
                dve.scalar_tensor_tensor(out=z_t[i % 2][:, :], in0=ring[i % 4], scalar=back[:, 1:2], in1=bfb[:, :],
                                         op0=ALU.mult, op1=ALU.add).then_inc(s_z, 1)

            for i in range(NT):
                for j in range(PER_FFN):
                    if todo:
                        max_part(0, todo.pop(0)[1])
                    if len(todo) == len(FIRST_MAXES) - NM and not negs.n:
                        for link in range(LINKS):
                            neg_part(0, link)
                    if j == 1 and i:
                        z_out(i - 1)
                if i == 0:
                    dve.wait_ge(s_bcat, 16 * (GROUPS + 2))
                    dve.memset(va[1][:, :, :, :].rearrange("p t h (d e) -> p (t h d) e", e=2)[:, :, 1], 1.0)
            z_out(NT - 1)
            dve.sem_inc(s_acc_free, 1)
            dve.wait_ge(s_g, NT)

            def step(trip, u, last):
                plan = Plan(u, last)
                for n in range(NU):
                    if n == CT:
                        acc_out(trip, 0)
                    todo = maxes_of(n, plan.near, plan.far)
                    for j in range(PER_UNIT):
                        if plan.neg and n == HALF_U:
                            for link in (0, 1) if j == 0 else (j + 1,):
                                neg_part(trip, link)
                        if todo:
                            max_part(trip, todo[j][1])
                    if last and u == 1 and n == HALF_U:
                        inverse(0)
                    if last and u == 2 and n == HALF_U:
                        inverse(1)
                        dve.sem_inc(s_col, 1)
                        over_row(1, 2)
                    if last and u == 2 and n == HALF_U + 1:
                        split_proj()
                    if last and u == 2 and n == HALF_U // 2:
                        dve.wait_ge(s_wp, 16)
                        largest_to(0, wp.rearrange("p k o -> p (k o)"))
                    if last and u == 3 and n in NORMAL_AT:
                        normalise(*NORMAL_AT[n])
                acc_out(trip, 1)

            def split_proj():
                dve.wait_ge(s_row, 2 * 2 + 2)
                dve.tensor_copy(bound[:, 4:5], mxp[0][:, P:P + 1]).then_inc(s_large, 1)
                link_large()
                scales(4, 5)
                dve.wait_ge(s_scale, 3)
                dve.tensor_scalar(back_proj[:, :], power[:, 3:4], power[:, 4:5], 1 / W_SCALE ** 2, ALU.mult, ALU.mult)
                dve.tensor_scalar(wpp[0], wp, scale[:, 4:5], None, ALU.mult).then_inc(s_large, 1)
                link_large()
                whole, hi, lo = (t.rearrange("p k o -> p (k o)") for t in (wp, *wpp))
                dve.scalar_tensor_tensor(out=lo, in0=whole, scalar=scale[:, 4:5], in1=hi,
                                         op0=ALU.mult, op1=ALU.subtract).then_inc(s_wpp, 1)

            def inverse(p):
                dve.wait_ge(s_sums, 16 * (p + 1))
                dve.reciprocal(inv[p], sums[p]).then_inc(s_inv, 1)

            normals = Tally()

            def normalise(p, j):
                b, dts = PARTS[p]
                dt = dts[j]
                dve.wait_ge(s_invb[p], 16 * len(dts))
                t, hi = (a[..., dt, b * SEQ:(b + 1) * SEQ] for a in (att[:, :, :], atp[:, 0]))
                dve.tensor_tensor(t, t, invb[b][dt], ALU.mult).then_inc(s_am, 1)
                normals.add()
                dve.wait_ge(s_am, normals.n)
                dve.tensor_scalar(t, t, scale[:, 3:4], bvs[:, dt:dt + 1], ALU.mult, ALU.add).then_inc(s_as, 1)
                if p < 2:
                    dve.wait_ge(s_as, normals.n)
                    dve.tensor_copy(hi, t).then_inc(s_athi, 1)

            with dve.Fori(0, DTS - 1, 1) as trip:
                for u in range(STEPS):
                    step(trip, u, False)
            more = DTS - 2
            maxed.n += NM * STEPS * more
            links.n += (LINKS - 1) * STEPS * more
            negs.n += STEPS * more
            pvs.n += NU * STEPS * more
            rawd.n += 32 * STEPS * more
            for u in range(STEPS):
                step(DTS - 1, u, True)

            inverse(2)
            dve.wait_ge(s_bp, 16)
            for i in range(NT):
                if i == 3:
                    normalise(2, 0)
                    dt, part = DTS - 1, slice(SEQ, 2 * SEQ)
                    dve.wait_ge(s_lasthi, 1)
                    dve.tensor_tensor(atp[:, 1, dt, part], att[:, dt, part], atp[:, 0, dt, part], ALU.subtract)\
                       .then_inc(s_last, 1)
                dve.wait_ge(s_op, i + 1)
                y, last = y_t[i % 2], xt[i // 4][:, i % 4, :]
                dve.scalar_tensor_tensor(out=y, in0=ring[i % 4], scalar=back_proj[:, 0:1], in1=bfb[:, :],
                                         op0=ALU.mult, op1=ALU.add).then_inc(s_y, 1)
                dve.wait_ge(s_y, i + 1)
                dve.wait_ge(s_xg[i // 4], 32)
                dve.tensor_tensor(y, y, gt[i // 4][:, i % 4, :], ALU.mult).then_inc(s_yg, 1)
                dve.wait_ge(s_yg, i + 1)
                dve.tensor_tensor(last, y, last, ALU.add).then_inc(s_res, 1)

        @block.gpsimd
        def _(pool):
            hi = Tally()
            mids = Tally()

            def split(trip):
                hi.add(CHUNKS)
                pool.wait_ge(s_hi, hi.at(trip, CHUNKS * STEPS))
                pool.tensor_tensor(pieces[:, 1, :], qk[:, :], pieces[:, 0, :], ALU.subtract).then_inc(s_mid, 1)
                mids.add()
                pool.wait_ge(s_mid, mids.at(trip, STEPS))
                pool.tensor_tensor(qk[:, :], qk[:, :], pieces[:, 0, :], ALU.subtract).then_inc(s_rest, 1)
                pool.wait_ge(s_rest, mids.at(trip, STEPS))
                pool.tensor_tensor(pieces[:, 2, :], qk[:, :], pieces[:, 1, :], ALU.subtract).then_inc(s_lo, 1)

            his = Tally()

            def last_pieces(i):
                for t in range(4):
                    pool.wait_ge(s_xhi, 4 * i + t + 1)
                    pool.tensor_tensor(xp[i][:, 1, t, :], xin[i][:, t, :], xp[i][:, 0, t, :], ALU.subtract)\
                        .then_inc(s_xlo, 1)

            def weights_split(trip, pieces_t, whole):
                his.add()
                pool.wait_ge(s_whi, his.at(trip, 3))
                flat = [t.rearrange("p k n -> p (k n)") for t in (whole[:, :, :], pieces_t[:, 0], pieces_t[:, 1])]
                pool.tensor_tensor(flat[2], flat[0], flat[1], ALU.subtract).then_inc(s_wlo, 1)

            last_pieces(0)
            last_pieces(1)
            weights_split(0, wqks[0], wqk[0])
            weights_split(0, wvs, wv)
            weights_split(0, wqks[1], wqk[1])
            last_pieces(2)
            last_pieces(3)
            split(0)
            weights_split(0, wfs, wf)
            split(0)
            split(0)

            def step(trip, u, last):
                if not last and u < 2:
                    weights_split(trip, wqks[u], wqk[u])
                if not last and u == 2:
                    weights_split(trip, wvs, wv)
                if Plan(u, last).qk:
                    split(trip)

            with pool.Fori(0, DTS - 1, 1) as trip:
                for u in range(STEPS):
                    step(trip, u, False)
            hi.n += CHUNKS * STEPS * (DTS - 2)
            his.n += 3 * (DTS - 2)
            mids.n += STEPS * (DTS - 2)
            for u in range(STEPS):
                step(DTS - 1, u, True)
            count = 0
            for b, dts in PARTS[:2]:
                for dt in dts:
                    count += 1
                    pool.wait_ge(s_athi, count)
                    part = slice(b * SEQ, (b + 1) * SEQ)
                    pool.tensor_tensor(atp[:, 1, dt, part], att[:, dt, part], atp[:, 0, dt, part], ALU.subtract)\
                        .then_inc(s_atlo, 1)


_INS = ["L0_attn_hidden_states", "L0_attn_w_attn", "L0_attn_b_attn", "L0_attn_w_proj", "L0_attn_b_proj",
        "L0_ffn_gate", "L0_ffn_kernel", "L0_ffn_bias", "L0_ffn_lora_A", "L0_ffn_lora_B",
        "L0_ffn_lora_A_shared", "L0_ffn_lora_B_shared"]


def _constants():
    import numpy as np

    bf = np.dtype("bfloat16")
    ident = np.eye(P, dtype=np.float32)
    mask = np.zeros((P, CH), np.float32)
    mask[:, CH - P:] = np.where(np.arange(P)[None, :] > np.arange(P)[:, None], np.float32(NEG), np.float32(0))
    maskb = np.where(np.arange(P)[:, None] > np.arange(P)[None, :], np.float32(-1e30), np.float32(0)).astype(bf)
    slopes = (np.float32(2 ** (-2 ** (-(5 - 3)))) ** np.arange(1, HEADS + 1, dtype=np.float32)).astype(np.float32)
    term = (slopes[:, None] * np.arange(SEQ, dtype=np.float32)[None, :] / np.float32(SCALE)).astype(np.float32)
    parts = []
    for _ in range(PIECES):
        part = term.astype(bf)
        parts.append(part)
        term = term - part.astype(np.float32)
    alibi = np.stack(parts, 1).reshape(HEADS // HG, HG, PIECES, SEQ).transpose(0, 2, 1, 3)
    pick = np.tile(np.eye(RANK, dtype=np.float32), (P // RANK, 1))
    return {"c_ident": ident, "c_ident16": ident.astype(np.float16), "c_identb": ident.astype(bf),
            "c_mask": mask, "c_maskb": maskb,
            "c_alibi": np.ascontiguousarray(alibi.reshape(HEADS // HG, PIECES, HG * SEQ)), "c_pick": pick,
            "c_ones": np.ones((2 * PIECES, HG, SEQ), bf)}


def _by_group(w, b):
    import numpy as np

    w = w.reshape(HID, 3, HEADS // HG, HG, HD)
    b = b.reshape(3, HEADS // HG, HG, HD)
    return {"w_qk": np.ascontiguousarray(w[:, :2].transpose(2, 0, 1, 4, 3).reshape(HEADS // HG, HID, P)),
            "b_qk": np.ascontiguousarray(b[:2].transpose(1, 0, 3, 2).reshape(HEADS // HG, P)),
            "w_v": np.ascontiguousarray(w[:, 2].reshape(HID, HID)),
            "b_v": np.ascontiguousarray(b[2].reshape(KT, P).T)}


def kernel(**inputs):
    import numpy as np
    import concourse.bacc as bacc
    from concourse.bass_utils import run_bass_kernel_spmd

    nc = bacc.Bacc("TRN2", target_bir_lowering=False, num_devices=1)
    arrays = {f"in_{name}": np.ascontiguousarray(inputs[name]) for name in _INS if "_attn_w_attn" not in name
              and "_attn_b_attn" not in name}
    arrays.update(_by_group(np.asarray(inputs["L0_attn_w_attn"]), np.asarray(inputs["L0_attn_b_attn"])))
    arrays.update(_constants())
    args = {name: nc.dram_tensor(name, a.shape, mybir.dt.from_np(a.dtype), kind="ExternalInput").ap()
            for name, a in arrays.items()}
    out = nc.dram_tensor("out", [TOK, HID], F32, kind="ExternalOutput").ap()
    flat = args["in_L0_attn_hidden_states"].rearrange("b s d -> (b s) d")
    rest = [args[f"in_{name}"] for name in _INS[3:]]
    constants = [args[f"c_{name}"] for name in ("ident", "ident16", "identb", "mask", "maskb", "alibi", "pick", "ones")]
    attention_and_gate(nc, flat, args["w_qk"], args["w_v"], args["b_qk"], args["b_v"], *rest, *constants, out)
    got = run_bass_kernel_spmd(nc, [arrays], core_ids=[0])
    return got.results[0]["out"].reshape(BATCH, SEQ, HID)
```
